# Optimizing a Trainium2 kernel written in Bass

```python
import numpy as np
import jax
import jax.numpy as jnp

def _softmax(x, axis=-1):
    return jax.nn.softmax(x, axis=axis)

def _gelu(x):
    return jax.nn.gelu(x, approximate=True)

def _silu(x):
    return jax.nn.silu(x)

def _sigmoid(x):
    return jax.nn.sigmoid(x)

def _layernorm(x, axis=-1, eps=1e-05):
    m = jnp.mean(x, axis=axis, keepdims=True)
    v = jnp.var(x, axis=axis, keepdims=True)
    return (x - m) / jnp.sqrt(v + eps)

def _scatter_add(tgt, idx, src, axis=0):
    return tgt.at[idx].add(src)

def _segment_sum(src, seg, n):
    return jax.ops.segment_sum(src, seg, n)
kernel_name = 'mk_flamingo_gated_d1_seqx_r4_5e74d6'

def setup_inputs(seed: int=0):
    np.random.seed(seed)
    _w = jnp.asarray

    def _rec_inputs():
        import jax
        import jax.numpy as jnp
        _rk = jax.random.key(seed)
        x = 0.0001212 + 1 * jax.random.normal(jax.random.fold_in(_rk, 1), (4, 512, 512), jnp.float32)
        _lenS = 512 - jax.random.randint(jax.random.fold_in(_rk, 7), (4,), 0, max(1, 512 // 4) + 1, jnp.int32)
        _lenS2 = 512 - jax.random.randint(jax.random.fold_in(_rk, 8), (4,), 0, max(1, 512 // 4) + 1, jnp.int32)
        _ctx_2048P = jax.random.normal(jax.random.fold_in(_rk, 11), (4, 16, 512), jnp.float32)
        _ctx_2048c = jax.random.dirichlet(jax.random.fold_in(_rk, 511), 0.3 * jnp.ones((16,), jnp.float32), (4, 512))
        _ctx_2048t = jnp.einsum('bsk,bkd->bsd', _ctx_2048c, _ctx_2048P)
        _ctx_2048t = _ctx_2048t * jax.lax.rsqrt(jnp.mean(jnp.square(_ctx_2048t)) + 1e-12) * 0.953939
        ctx_2048 = 0.000173663 + 1.0001 * (_ctx_2048t + 0.3 * jax.random.normal(jax.random.fold_in(_rk, 611), (4, 512, 512), jnp.float32))
        _g = jax.random.normal(jax.random.fold_in(_rk, 9001), (2, 1), jnp.float32)
        _g = jnp.sign(_g) * jnp.maximum(jnp.abs(_g), 1.0) + (_g == 0) * 1.0
        g_xattn = _g[0]
        g_ffn = _g[1]
        return (x, ctx_2048, g_xattn, g_ffn)
    x, ctx_2048, g_xattn, g_ffn = _rec_inputs()

    def _L0_xattn_setup():
        import jax, jax.numpy as jnp
        import numpy as np
        B_DIM, T_DIM, C_DIM = (16, 256, 512)

        def _wkv(w, u, k, v):
            Bn, Tn, Cn = k.shape
            NEG_INF = jnp.float32(-1e+38)

            def step(carry, kv_t):
                p, q, o = carry
                kt, vt = kv_t
                no = jnp.maximum(o, u + kt)
                A = jnp.exp(o - no)
                E = jnp.exp(u + kt - no)
                y = (A * p + E * vt) / (A * q + E)
                no2 = jnp.maximum(w + o, kt)
                A2 = jnp.exp(w + o - no2)
                E2 = jnp.exp(kt - no2)
                return ((A2 * p + E2 * vt, A2 * q + E2, no2), y)
            init = (jnp.zeros((Bn, Cn), k.dtype), jnp.zeros((Bn, Cn), k.dtype), jnp.full((Bn, Cn), NEG_INF, k.dtype))
            kT = jnp.moveaxis(k, 1, 0)
            vT = jnp.moveaxis(v, 1, 0)
            _, yT = jax.lax.scan(step, init, (kT, vT))
            return jnp.moveaxis(yT, 0, 1)
        key = jax.random.key(seed)
        k1, k2, k3, k4 = jax.random.split(key, 4)
        w = -jnp.exp(jax.random.normal(k1, (C_DIM,), jnp.float32))
        u = jax.random.normal(k2, (C_DIM,), jnp.float32)
        k = jax.random.normal(k3, (B_DIM, T_DIM, C_DIM), jnp.float32)
        v = jax.random.normal(k4, (B_DIM, T_DIM, C_DIM), jnp.float32)
        return {'B': B_DIM, 'T': T_DIM, 'C': C_DIM, 'w': w, 'u': u, 'k': k, 'v': v}
    _L0_xattn_all = _L0_xattn_setup()
    _L0_xattn_in = {k: v for k, v in _L0_xattn_all.items() if k in ('w', 'u')}
    del _L0_xattn_all

    def _L0_ffn_setup():
        import jax, jax.numpy as jnp
        import numpy as np
        B_, S, D = (2, 512, 512)
        F_ = 2048
        R = 16
        H = 16
        HD = D // H
        MOD_SCALE = 0.1
        EPS = 1e-06

        def _rmsnorm(x, w):
            v = jnp.mean(x * x, axis=-1, keepdims=True)
            return x * jax.lax.rsqrt(v + EPS) * w

        def _attention(x, Wq, Wk, Wv, Wo):
            b, s, d = x.shape
            q = (x @ Wq.T).reshape(b, s, H, HD)
            k = (x @ Wk.T).reshape(b, s, H, HD)
            v = (x @ Wv.T).reshape(b, s, H, HD)
            scores = jnp.einsum('bqhd,bkhd->bhqk', q, k) / np.sqrt(HD).astype(np.float32)
            causal = jnp.tril(jnp.ones((s, s), bool))
            scores = jnp.where(causal, scores, jnp.finfo(scores.dtype).min)
            probs = jax.nn.softmax(scores, axis=-1)
            out = jnp.einsum('bhqk,bkhd->bqhd', probs, v).reshape(b, s, d)
            return out @ Wo.T
        key = jax.random.key(seed)
        ks = jax.random.split(key, 12)
        sd = 0.02
        return {'hidden_states': jax.random.normal(ks[0], (B_, S, D), jnp.float32), 'ln1_w': jnp.ones((D,), jnp.float32), 'ln2_w': jnp.ones((D,), jnp.float32), 'Wq': jax.random.normal(ks[1], (D, D), jnp.float32) * sd, 'Wk': jax.random.normal(ks[2], (D, D), jnp.float32) * sd, 'Wv': jax.random.normal(ks[3], (D, D), jnp.float32) * sd, 'Wo': jax.random.normal(ks[4], (D, D), jnp.float32) * sd, 'A': jax.random.normal(ks[5], (D, R), jnp.float32) * (0.01 / np.sqrt(D)), 'B': jax.random.normal(ks[6], (R, F_), jnp.float32) * (0.01 / np.sqrt(R)), 'W_in_base': jax.random.normal(ks[7], (F_, D), jnp.float32) * sd, 'W_up_base': jax.random.normal(ks[8], (F_, D), jnp.float32) * sd, 'W_down': jax.random.normal(ks[9], (D, F_), jnp.float32) * sd}
    _L0_ffn_all = _L0_ffn_setup()
    _L0_ffn_in = {k: v for k, v in _L0_ffn_all.items() if k in ('ln1_w', 'ln2_w', 'Wq', 'Wk', 'Wv', 'Wo', 'A', 'B', 'W_in_base', 'W_up_base', 'W_down')}
    del _L0_ffn_all
    return {'x': x, 'ctx_2048': ctx_2048, 'g_xattn': g_xattn, 'g_ffn': g_ffn, 'L0_xattn_w': _L0_xattn_in['w'], 'L0_xattn_u': _L0_xattn_in['u'], 'L0_ffn_ln1_w': _L0_ffn_in['ln1_w'], 'L0_ffn_ln2_w': _L0_ffn_in['ln2_w'], 'L0_ffn_Wq': _L0_ffn_in['Wq'], 'L0_ffn_Wk': _L0_ffn_in['Wk'], 'L0_ffn_Wv': _L0_ffn_in['Wv'], 'L0_ffn_Wo': _L0_ffn_in['Wo'], 'L0_ffn_A': _L0_ffn_in['A'], 'L0_ffn_B': _L0_ffn_in['B'], 'L0_ffn_W_in_base': _L0_ffn_in['W_in_base'], 'L0_ffn_W_up_base': _L0_ffn_in['W_up_base'], 'L0_ffn_W_down': _L0_ffn_in['W_down']}

def reference(x, ctx_2048, g_xattn, g_ffn, L0_xattn_w, L0_xattn_u, L0_ffn_ln1_w, L0_ffn_ln2_w, L0_ffn_Wq, L0_ffn_Wk, L0_ffn_Wv, L0_ffn_Wo, L0_ffn_A, L0_ffn_B, L0_ffn_W_in_base, L0_ffn_W_up_base, L0_ffn_W_down):
    import jax
    import jax.numpy as jnp

    def _L0_xattn_ref(B, T, C, w, u, k, v):
        import jax, jax.numpy as jnp
        import numpy as np
        B_DIM, T_DIM, C_DIM = (16, 256, 512)

        def _wkv(w, u, k, v):
            Bn, Tn, Cn = k.shape
            NEG_INF = jnp.float32(-1e+38)

            def step(carry, kv_t):
                p, q, o = carry
                kt, vt = kv_t
                no = jnp.maximum(o, u + kt)
                A = jnp.exp(o - no)
                E = jnp.exp(u + kt - no)
                y = (A * p + E * vt) / (A * q + E)
                no2 = jnp.maximum(w + o, kt)
                A2 = jnp.exp(w + o - no2)
                E2 = jnp.exp(kt - no2)
                return ((A2 * p + E2 * vt, A2 * q + E2, no2), y)
            init = (jnp.zeros((Bn, Cn), k.dtype), jnp.zeros((Bn, Cn), k.dtype), jnp.full((Bn, Cn), NEG_INF, k.dtype))
            kT = jnp.moveaxis(k, 1, 0)
            vT = jnp.moveaxis(v, 1, 0)
            _, yT = jax.lax.scan(step, init, (kT, vT))
            return jnp.moveaxis(yT, 0, 1)
        return _wkv(w, u, k, v)

    def _L0_ffn_ref(hidden_states, ln1_w, ln2_w, Wq, Wk, Wv, Wo, A, B, W_in_base, W_up_base, W_down):
        import jax, jax.numpy as jnp
        import numpy as np
        B_, S, D = (2, 512, 512)
        F_ = 2048
        R = 16
        H = 16
        HD = D // H
        MOD_SCALE = 0.1
        EPS = 1e-06

        def _rmsnorm(x, w):
            v = jnp.mean(x * x, axis=-1, keepdims=True)
            return x * jax.lax.rsqrt(v + EPS) * w

        def _attention(x, Wq, Wk, Wv, Wo):
            b, s, d = x.shape
            q = (x @ Wq.T).reshape(b, s, H, HD)
            k = (x @ Wk.T).reshape(b, s, H, HD)
            v = (x @ Wv.T).reshape(b, s, H, HD)
            scores = jnp.einsum('bqhd,bkhd->bhqk', q, k) / np.sqrt(HD).astype(np.float32)
            causal = jnp.tril(jnp.ones((s, s), bool))
            scores = jnp.where(causal, scores, jnp.finfo(scores.dtype).min)
            probs = jax.nn.softmax(scores, axis=-1)
            out = jnp.einsum('bhqk,bkhd->bqhd', probs, v).reshape(b, s, d)
            return out @ Wo.T
        residual = hidden_states
        x = _rmsnorm(hidden_states, ln1_w)
        attn = _attention(x, Wq, Wk, Wv, Wo)
        mod = MOD_SCALE * jnp.tanh(attn @ A)
        h = _rmsnorm(residual, ln2_w)
        gate_pre = h @ W_in_base.T + mod * (h @ A) @ B
        gate = jax.nn.silu(gate_pre)
        up = h @ W_up_base.T
        mlp_out = gate * up @ W_down.T
        return residual + mlp_out
    x = x + jnp.tanh(g_xattn[0]) * _L0_xattn_ref(4, 512, 512, L0_xattn_w, L0_xattn_u, _layernorm(x, axis=-1), ctx_2048)
    x = x + jnp.tanh(g_ffn[0]) * _L0_ffn_ref(_layernorm(x, axis=-1), L0_ffn_ln1_w, L0_ffn_ln2_w, L0_ffn_Wq, L0_ffn_Wk, L0_ffn_Wv, L0_ffn_Wo, L0_ffn_A, L0_ffn_B, L0_ffn_W_in_base, L0_ffn_W_up_base, L0_ffn_W_down)
    return x

_drawn_inputs = setup_inputs


def setup_inputs(seed=0):
    import zlib

    import numpy as np

    out = dict(_drawn_inputs(seed))
    spreads = {'L0_ffn_ln1_w': (1.0, 0.6), 'L0_ffn_ln2_w': (1.0, 0.2)}
    factors = {'L0_ffn_Wq': 64.0,
     'L0_ffn_Wk': 64.0,
     'L0_ffn_Wv': 64.0,
     'L0_ffn_Wo': 64.0,
     'L0_ffn_A': 64.0,
     'L0_ffn_B': 64.0}
    for name, (base, spread) in spreads.items():
        noise = np.random.default_rng([zlib.crc32(name.encode()), seed]).standard_normal(out[name].shape)
        drawn = base * np.exp(spread * noise) if base else spread * noise
        out[name] = jnp.asarray(drawn.astype(out[name].dtype))
    for name, factor in factors.items():
        out[name] = (out[name] * factor).astype(out[name].dtype)
    return out
```

```python
from contextlib import ExitStack

import numpy as np

import concourse.bass as bass
import concourse.mybir as mybir

F32, F32R, BF16 = mybir.dt.float32, mybir.dt.float32r, mybir.dt.bfloat16
ALU, ACT, AX = mybir.AluOpType, mybir.ActivationFunctionType, mybir.AxisListType

NB, T, D = 4, 512, 512
FF, R, H = 2048, 16, 16
HD = D // H
P = 128
TB, DB = T // P, D // P
NF = FF // P
G = H // 4
VW = 32
GA = H * R + R
LN_EPS, RMS_EPS = 1e-5, 1e-6
MASKED = -1e30
SM_SCALE = float(1.0 / np.sqrt(np.float32(HD)))
MOD_SCALE = 0.1
BONUS_LOW, SHIFT_LOW = -70.0, -40.0
DGE_SCRATCH = 1024
DVE_OWN_PER_BATCH = 64

E_AT = [0, 640, 1024, 512]
S_STEPS = [[(0, 3)], [(P, 2), (0, 0)], [(0, 1)]]
ST_STEPS = [[(0, 0)], [(P, 1), (0, 3)], [(0, 2)]]
ST_E = [(0, 512), (512, 512), (1024, 256)]


def flamingo_layer(nc, x, ctxT, w4, u4, gates, ln1, ln2, wqT, wkT, wv, wo, a4, b_mod, w_gu, w_down, out):
    es = ExitStack()
    with es:
        top = [nc.sbuf_base + (-nc.sbuf_base) % 64]

        def place(name, shape, dt, at=None):
            size = int(np.prod(shape[1:])) * (2 if dt == BF16 else 4)
            size += -size % 64
            off = top[0] if at is None else at[0]
            if at is None:
                top[0] += size
            else:
                at[0] += size
                assert at[0] <= at[1], name
            return nc.alloc_sbuf_tensor_at(name, shape, dt, offset=off)

        def region(size):
            at = top[0]
            top[0] += size
            return [at, at + size]

        def sem(name):
            return es.enter_context(nc.semaphore(name))

        ident = place("ident", [P, P], F32)
        identb = place("identb", [P, P], BF16)
        mask_qk = place("mask_qk", [P, P], BF16)
        mask_kq = place("mask_kq", [P, P], BF16)
        steps = place("steps", [P, T], F32)
        w_sb = place("w_sb", [P, DB], F32)
        u_sb = place("u_sb", [P, DB], F32)
        gates_sb = place("gates_sb", [P, 2], F32)
        ln1_sb = place("ln1_sb", [P, DB], F32)
        ln2_sb = place("ln2_sb", [P, DB], F32)
        a_sb = place("a_sb", [P, DB, R], F32)
        neg_wp = place("neg_wp", [P, DB], F32)
        w_minus = place("w_minus", [P, DB], F32)
        decay = place("decay", [P, DB], F32)
        bonus = place("bonus", [P, DB], F32)
        shift = place("shift", [P, DB], F32)
        rho = place("rho", [P, DB], F32)
        gate_t = place("gate_t", [P, 2], F32)
        half_gate = place("half_gate", [P, 1], F32)
        minus_half = place("minus_half", [P, TB], F32)
        wq_s = [place(f"wq_{n}", [P, DB, D], F32R) for n in ("hi", "lo")]
        wk_s = [place(f"wk_{n}", [P, DB, D], F32R) for n in ("hi", "lo")]
        ga_s = [place(f"ga_{n}", [P, DB, GA], F32R) for n in ("hi", "lo")]
        b_s = place("b_s", [5 * R, FF], F32R)
        v_aug = place("v_aug", [P, TB, H, VW], F32)
        k_st = [place(f"k_st{i}", [P, 4, T], F32R) for i in range(3)]
        x_sb = place("x_sb", [P, TB, D], F32)
        base_at = region(8192)
        raw_b = place("raw_b", [5 * R, FF], F32, list(base_at))
        base = place("base", [P, TB, D], F32, base_at)
        h_s = [place(f"h_{n}", [P, DB, T], F32R) for n in ("hi", "lo")]
        raw_gu = [place(f"raw_gu{i}", [P, 2 * D], F32) for i in range(2)]
        raw_d = [place(f"raw_d{i}", [P, D], F32) for i in range(2)]
        out_sb = [place(f"out_sb{i}", [P, D], F32) for i in range(2)]
        bn6 = place("bn6", [P, TB, 6], F32)
        mean = place("mean", [P, TB], F32)
        var = place("var", [P, TB], F32)
        half_diff = place("half_diff", [P, TB], F32)
        var_eps = place("var_eps", [P, TB], F32)
        rstd = place("rstd", [P, TB], F32)
        bn6b = place("bn6b", [P, TB, 6], F32)
        meanb = place("meanb", [P, TB], F32)
        varb = place("varb", [P, TB], F32)
        var_epsb = place("var_epsb", [P, TB], F32)
        rstdb = place("rstdb", [P, TB], F32)
        vr = place("vr", [P, TB], F32)
        ms_eps = place("ms_eps", [P, TB], F32)
        rms = place("rms", [P, TB], F32)
        hn_scale = place("hn_scale", [P, TB], F32)
        gr = place("gr", [P, TB], F32)
        base_mul = place("base_mul", [P, TB], F32)
        base_add = place("base_add", [P, TB], F32)
        mx = place("mx", [P, TB, 4], F32)
        nmc = place("nmc", [P, TB, 8], F32)
        nmrow = place("nmrow", [8, T], F32R)
        pvs = place("pvs", [P, T], F32)
        rl = place("rl", [P, TB, 4], F32)
        pvn = place("pvn", [P, TB, 4, R], F32)
        modp = place("modp", [P, G, TB, R], F32)
        modsum = place("modsum", [P, TB, R], F32)
        modt = place("modt", [P, TB, R], F32)
        h_a = place("h_a", [P, TB, R], F32)
        t_mod = place("t_mod", [P, TB, R], F32)
        tcols = place("tcols", [P, TB, 5 * R], F32)
        t_s = place("t_s", [5 * R, T], F32R)

        norm_at = region(8192)
        norm = place("norm", [P, TB, D], F32, norm_at)
        r2 = region(24576)
        r2a, r2s = list(r2), list(r2)
        hn_s = [place(f"hn_{n}", [P, DB, T], F32R, r2a) for n in ("hi", "lo")]
        raw_wq = place("raw_wq", [P, DB, D], F32, r2s)
        raw_wk = place("raw_wk", [P, DB, D], F32, r2s)
        raw_wv = place("raw_wv", [P, DB, D], F32, r2s)
        gu_s = [[place(f"gu{i}_{n}", [P, 2 * D], F32R, r2) for n in ("hi", "lo")] for i in range(2)]
        wd_s = [[place(f"wd{i}_{n}", [P, D], F32R, r2) for n in ("hi", "lo")] for i in range(2)]
        r1 = region(45056)
        r1a = list(r1)
        q_st = [place(f"q_st{i}", [P, 4, T], F32R, r1a) for i in range(3)]
        e_row = place("e_row", [P, 4, 1280], F32, r1a)
        vT = place("vT", [P, DB, T], F32, r1)
        kexp = [place(f"kexp{i}", [P, T], F32, r1) for i in range(2)]
        kv = [place(f"kv{i}", [P, T], F32, r1) for i in range(2)]
        p_run = place("p_run", [P, T + 1], F32, r1)
        q_run = place("q_run", [P, T + 1], F32, r1)
        yT = place("yT", [P, DB, T], F32, r1)
        r1s = list(r1)
        raw_wo = place("raw_wo", [P, DB, D], F32, r1s)
        woa = place("woa", [P, DB, 4 * R], F32, r1s)
        th = place("th", [P, T], F32, r1)
        gsil = place("gsil", [P, T], F32, r1)
        prod = place("prod", [P, T], F32, r1)
        act_s = [[place(f"act{i}_{n}", [P, T], F32R, r1) for n in ("hi", "lo")] for i in range(2)]
        assert top[0] <= nc.sbuf_usable_end, (top[0], nc.sbuf_usable_end)

        ps = es.enter_context(nc.psum_tensor("ps", [P, 8, 512], F32))
        TPB = 7

        w_ld, woa_ld, b_ld = sem("w_ld"), sem("woa_ld"), sem("b_ld")
        small_ld, x_ld, v_ld = sem("small_ld"), sem("x_ld"), sem("v_ld")
        gu_ld = [sem(f"gu_ld{i}") for i in range(2)]
        d_ld = [sem(f"d_ld{i}") for i in range(2)]
        rep_ld = [sem(f"rep_ld{i}") for i in range(G)]
        nm_ld = [sem(f"nm_ld{i}") for i in range(G)]
        out_st = [sem(f"out_st{i}") for i in range(2)]
        const_rdy, prep_rdy, pool_own = sem("const_rdy"), sem("prep_rdy"), sem("pool_own")
        decay_rdy, ones_rdy = sem("decay_rdy"), sem("ones_rdy")
        woa_ps, ga_ps, woa_sb, wsplit_hi, wsplit_lo = (sem(n) for n in ("woa_ps", "ga_ps", "woa_sb", "wsplit_hi", "wsplit_lo"))
        stats1, rstd1, xn_rdy, xnT_ps, kt_rdy, kexp_rdy, kv_rdy, yT_rdy, yT_ps, x1_rdy = (sem(n) for n in (
            "stats1", "rstd1", "xn_rdy", "xnT_ps", "kt_rdy", "kexp_rdy", "kv_rdy", "yT_rdy", "yT_ps", "x1_rdy"))
        stats2, rstd2, ms2, rms2, hn_rdy, base_rdy, hnT_ps, hT_hi, hT_lo = (sem(n) for n in (
            "stats2", "rstd2", "ms2", "rms2", "hn_rdy", "base_rdy", "hnT_ps", "hT_hi", "hT_lo"))
        qk_ps, qk_hi, qk_lo, va_ps, va_sb, s_ps, smax_rdy, nmc_rdy, nm_ps, nmrow_rdy = (sem(n) for n in (
            "qk_ps", "qk_hi", "qk_lo", "va_ps", "va_sb", "s_ps", "smax_rdy", "nmc_rdy", "nm_ps", "nmrow_rdy"))
        st_ps, exp_rdy, pv_ps, pvs_rdy, pvT_ps, pvT_used, modsum_rdy, modt_rdy, t_rdy, tT_ps, tT_rdy = (sem(n) for n in (
            "st_ps", "exp_rdy", "pv_ps", "pvs_rdy", "pvT_ps", "pvT_used", "modsum_rdy", "modt_rdy", "t_rdy", "tT_ps", "tT_rdy"))
        gu_hi, gu_lo, wd_hi, wd_lo, gate_ps, up_ps, down_ps, th_rdy, prod_rdy, act_hi, act_lo, fin_rdy = (sem(n) for n in (
            "gu_hi", "gu_lo", "wd_hi", "wd_lo", "gate_ps", "up_ps", "down_ps", "th_rdy", "prod_rdy", "act_hi", "act_lo", "fin_rdy"))
        dve_own = sem("dve_own")

        f32 = lambda ap: ap.bitcast(F32)
        blk = lambda i: slice(i * P, (i + 1) * P)
        quad = lambda j: slice(32 * j, 32 * j + 32)

        block = es.enter_context(nc.Block())

        @block.sync
        def _(sp):
            def load_x(n):
                sp.dma_start(x_sb[:], x[bass.ds(n, 1), :, :].rearrange("o (tb p) d -> p (o tb) d", p=P)).then_inc(x_ld, 16)

            def load_v(n):
                sp.dma_start(vT[:], ctxT[bass.ds(n, 1), :, :].rearrange("o (cb p) t -> p (o cb) t", p=P)).then_inc(v_ld, 16)

            def load_gu(f):
                sp.dma_start(raw_gu[f % 2][:], w_gu[f]).then_inc(gu_ld[f % 2], 16)

            def load_d(f):
                sp.dma_start(raw_d[f % 2][:], w_down[blk(f), :]).then_inc(d_ld[f % 2], 16)

            load_x(0)
            for dst, src in ((w_sb, w4), (u_sb, u4), (gates_sb, gates), (ln1_sb, ln1), (ln2_sb, ln2)):
                sp.dma_start(dst[:], src).then_inc(small_ld, 16)
            load_v(0)
            sp.dma_start(raw_wo[:], wo.rearrange("(ot p) j -> p ot j", p=P)).then_inc(woa_ld, 16)
            sp.dma_start(a_sb[:], a4.rearrange("(ot p) r -> p ot r", p=P)).then_inc(woa_ld, 16)
            sp.dma_start(raw_wv[:], wv.rearrange("(jt p) d -> p jt d", p=P)).then_inc(woa_ld, 16)
            sp.dma_start(raw_wq[:], wqT.rearrange("(db p) j -> p db j", p=P)).then_inc(w_ld, 16)
            sp.dma_start(raw_wk[:], wkT.rearrange("(db p) j -> p db j", p=P)).then_inc(w_ld, 16)
            sp.wait_ge(const_rdy, 2)
            for row in (0, 2 * R, 4 * R):
                sp.dma_start(raw_b[row:row + R, :], b_mod).then_inc(b_ld, 16)
            for f in range(2):
                load_gu(f)
                load_d(f)

            def batch(b, last):
                def replicate(g):
                    sp.wait_ge(qk_hi, b * 8 * G + 8 * g + 4)
                    sp.dma_start(f32(q_st[g % 3][64:96, :, :]), f32(q_st[g % 3][0:32, :, :])).then_inc(rep_ld[g], 16)
                    sp.wait_ge(qk_hi, b * 8 * G + 8 * g + 8)
                    sp.dma_start(f32(k_st[g % 3][32:64, :, :]), f32(k_st[g % 3][0:32, :, :])).then_inc(rep_ld[g], 16)

                def maxima(g):
                    sp.wait_ge(nmrow_rdy, b * G + g + 1)
                    for c in range(2):
                        sp.dma_start(f32(q_st[g % 3][96 + c:97 + c, :, :]), f32(nmrow[4 * c:4 * c + 4, :])).then_inc(nm_ld[g], 16)

                replicate(0)
                replicate(1)
                if not last:
                    sp.wait_ge(base_rdy, b + 1)
                    load_x(b + 1)
                maxima(0)
                replicate(2)
                maxima(1)
                replicate(3)
                maxima(2)
                maxima(3)
                for f in (2, 3):
                    sp.wait_ge(gu_lo, b * NF + f - 1)
                    load_gu(f)
                sp.wait_ge(wd_lo, b * NF + 1)
                load_d(2)
                if not last:
                    sp.wait_ge(pv_ps, (b + 1) * G)
                    load_v(b + 1)
                for f in range(NF):
                    if f + 4 < NF + 2 and not (last and f + 4 >= NF):
                        sp.wait_ge(gu_lo, b * NF + f + 3)
                        load_gu((f + 4) % NF)
                    if f + 3 < NF + 2 and not (last and f + 3 >= NF):
                        sp.wait_ge(wd_lo, b * NF + f + 2)
                        load_d((f + 3) % NF)
                for tb in range(TB):
                    sp.wait_ge(fin_rdy, b * TB + tb + 1)
                    sp.dma_start(out[bass.ds(b, 1), blk(tb), :].rearrange("o p d -> (o p) d"), out_sb[tb % 2][:]).then_inc(out_st[tb % 2], 16)

            with sp.Fori(0, NB - 1) as b:
                batch(b, False)
            batch(NB - 1, True)
            for i in range(2):
                sp.wait_ge(out_st[i], 16 * NB * TB // 2)

        @block.gpsimd
        def _(pool):
            pool.memset(b_clear := f32(raw_b[:]), 0.0).then_inc(const_rdy, 1)
            pool.memset(ident[:], 0.0).then_inc(pool_own, 1)
            pool.memset(mask_qk[:], 0.0).then_inc(pool_own, 1)
            pool.memset(mask_kq[:], 0.0).then_inc(pool_own, 1)
            pool.memset(minus_half[:], -0.5).then_inc(const_rdy, 1)
            pool.wait_ge(pool_own, 3)
            pool.affine_select(out=ident[:], in_=ident[:], compare_op=ALU.not_equal, fill=1.0, base=0,
                               pattern=[[-1, P]], channel_multiplier=1).then_inc(pool_own, 1)
            pool.affine_select(out=mask_qk[:], in_=mask_qk[:], compare_op=ALU.is_ge, fill=MASKED, base=0,
                               pattern=[[-1, P]], channel_multiplier=1).then_inc(const_rdy, 1)
            pool.affine_select(out=mask_kq[:], in_=mask_kq[:], compare_op=ALU.is_ge, fill=MASKED, base=0,
                               pattern=[[1, P]], channel_multiplier=-1).then_inc(const_rdy, 1)
            pool.iota(steps[:], [[1, T]], base=0, channel_multiplier=0,
                      allow_small_or_imprecise_dtypes=True).then_inc(const_rdy, 1)
            pool.wait_ge(pool_own, 4)
            pool.tensor_copy(identb[:], ident[:]).then_inc(const_rdy, 1)
            pool.memset(v_aug[:], 0.0).then_inc(pool_own, 1)
            pool.wait_ge(pool_own, 5)
            pool.memset(v_aug[:, :, :, R:R + 1], 1.0).then_inc(const_rdy, 1)
            pool.memset(tcols[:], 0.0).then_inc(const_rdy, 1)

            def recurrence(n):
                pool.wait_ge(stats1, n + 1)
                pool.tensor_tensor(rstd[:], var_eps[:], minus_half[:], ALU.pow).then_inc(rstd1, 1)
                for cb in range(DB):
                    if cb == 0:
                        pool.wait_ge(v_ld, 16 * (n + 1))
                    pool.wait_ge(kexp_rdy, n * DB + cb + 1)
                    if cb >= 2:
                        pool.wait_ge(yT_rdy, n * DB + cb - 1)
                    pool.tensor_tensor(kv[cb % 2][:], kexp[cb % 2][:], vT[:, cb, :], ALU.mult).then_inc(kv_rdy, 1)
                pool.wait_ge(stats2, n + 1)
                pool.tensor_tensor(rstdb[:], var_epsb[:], minus_half[:], ALU.pow).then_inc(rstd2, 1)
                pool.wait_ge(ms2, n + 1)
                pool.tensor_tensor(rms[:], ms_eps[:], minus_half[:], ALU.pow).then_inc(rms2, 1)

            recurrence(0)
            with pool.Fori(0, NB - 1) as b:
                recurrence(b + 1)

        @block.scalar
        def _(act):
            act.wait_ge(prep_rdy, 1)
            act.activation(decay[:], w_minus[:], ACT.Exp)
            act.activation(rho[:], bonus[:], ACT.Exp, scale=-1.0)
            act.activation(gate_t[:], gates_sb[:], ACT.Tanh).then_inc(decay_rdy, 1)

            def kexp_step(n, cb):
                act.wait_ge(kt_rdy, n * DB + cb + 1)
                act.activation(kexp[cb % 2][:], kexp[cb % 2][:], ACT.Exp, bias=shift[:, cb:cb + 1]).then_inc(kexp_rdy, 1)

            act.wait_ge(w_ld, 32)
            for raw, dst in ((raw_wq, wq_s), (raw_wk, wk_s)):
                for db in range(DB):
                    act.activation(dst[0][:, db, :], raw[:, db, :], ACT.Copy, scale=ln1_sb[:, db:db + 1]).then_inc(wsplit_hi, 1)
            act.wait_ge(b_ld, 48)
            act.activation(b_s[:], raw_b[:], ACT.Copy).then_inc(wsplit_hi, 1)
            for cb in range(DB):
                kexp_step(0, cb)
            act.wait_ge(ga_ps, 1)
            for db in range(DB):
                act.activation(ga_s[0][:, db, 0:H * R], ps[:, 5 + db // 2, 256 * (db % 2):256 * (db % 2) + 256], ACT.Copy,
                               scale=ln1_sb[:, db:db + 1])
                act.activation(ga_s[0][:, db, H * R:GA], a_sb[:, db, :], ACT.Copy, scale=ln2_sb[:, db:db + 1]).then_inc(wsplit_hi, 1)

            def split_gu(b, f):
                act.wait_ge(gu_ld[f % 2], (b * NF + f - f % 2) * 8 + 16)
                if f >= 2:
                    act.wait_ge(up_ps, b * NF + f - 1)
                act.activation(gu_s[f % 2][0][:], raw_gu[f % 2][:], ACT.Copy).then_inc(gu_hi, 1)

            def split_d(b, f):
                act.wait_ge(d_ld[f % 2], (b * NF + f - f % 2) * 8 + 16)
                if f >= 2:
                    act.wait_ge(down_ps, b * NF + f - 1)
                act.activation(wd_s[f % 2][0][:], raw_d[f % 2][:], ACT.Copy).then_inc(wd_hi, 1)

            def batch(b, last):
                for db in range(DB):
                    act.wait_ge(hnT_ps, b * DB + db + 1)
                    act.activation(hn_s[0][:, db, :], ps[:, 4 + db, :], ACT.Copy)
                    act.activation(h_s[0][:, db, :], ps[:, 4 + db, :], ACT.Copy, scale=ln2_sb[:, db:db + 1]).then_inc(hT_hi, 1)

                def qk_round(g):
                    for i, st in ((0, q_st), (1, k_st)):
                        act.wait_ge(qk_ps, b * 2 * G + 2 * g + i + 1)
                        if g >= 3 and i == 0:
                            act.wait_ge(st_ps, b * 6 * G + 6 * (g - 2))
                        for j in range(4):
                            act.activation(st[g % 3][0:32, j, :], ps[quad(j), 4 + i, :], ACT.Copy).then_inc(qk_hi, 1)

                def exps(g, s, pr):
                    k = 6 * g + 2 * s + pr
                    act.wait_ge(st_ps, b * 6 * G + k + 1)
                    if s == 0 and pr == 0 and g >= 1:
                        act.wait_ge(pv_ps, b * G + g)
                    at, width = ST_E[s]
                    act.activation(e_row[:, 2 * pr:2 * pr + 2, at:at + width], ps[:, 2:4, 0:width], ACT.Exp,
                                   scale=SM_SCALE).then_inc(exp_rdy, 1)

                qk_round(0)
                for tb in range(TB):
                    act.wait_ge(va_ps, b * TB + tb + 1)
                    act.activation(v_aug[:, tb, :, 0:R], ps[:, 6 + tb % 2, 0:H * R].rearrange("p (h r) -> p h r", r=R), ACT.Copy)
                    act.activation(h_a[:, tb, :], ps[:, 6 + tb % 2, H * R:GA], ACT.Copy).then_inc(va_sb, 1)
                qk_round(1)
                for g in range(G + 1):
                    for k in range(6):
                        if g >= 1:
                            exps(g - 1, k // 2, k % 2)
                        if k == 3 and 1 <= g and g + 1 < G:
                            qk_round(g + 1)
                split_gu(b, 0)
                split_gu(b, 1)
                split_d(b, 0)
                act.wait_ge(modsum_rdy, b + 1)
                act.activation(modt[:], modsum[:], ACT.Tanh).then_inc(modt_rdy, 1)
                for f in range(NF):
                    act.wait_ge(gate_ps, b * NF + f + 1)
                    if f == 0:
                        act.wait_ge(pv_ps, (b + 1) * G)
                    act.activation(th[:], ps[:, 4 + (2 * f) % 3, :], ACT.Tanh, scale=0.5).then_inc(th_rdy, 1)
                    act.wait_ge(prod_rdy, b * NF + f + 1)
                    if f >= 2:
                        act.wait_ge(down_ps, b * NF + f - 1)
                    act.activation(act_s[f % 2][0][:], prod[:], ACT.Copy).then_inc(act_hi, 1)
                    if f + 2 < NF:
                        split_gu(b, f + 2)
                    if f + 1 < NF:
                        split_d(b, f + 1)
                    if not last and f in range(2, 2 + 2 * DB, 2):
                        kexp_step(b + 1, f // 2 - 1)

            with act.Fori(0, NB - 1) as b:
                batch(b, False)
            batch(NB - 1, True)

        @block.vector
        def _(dve):
            own = {"base": 0, "n": 0}

            def mine(op):
                own["n"] += 1
                op.then_inc(dve_own, 1)

            def settled():
                dve.wait_ge(dve_own, own["base"] + own["n"])

            for i in range(3):
                dve.memset(f32(k_st[i][96:98, :, :]), 1.0).then_inc(ones_rdy, 1)
            dve.wait_ge(small_ld, 80)
            mine(dve.tensor_scalar(neg_wp[:], w_sb[:], 0.0, -1.0, ALU.max, ALU.mult))
            mine(dve.tensor_scalar(w_minus[:], w_sb[:], 0.0, None, ALU.min))
            settled()
            mine(dve.tensor_tensor(bonus[:], u_sb[:], neg_wp[:], ALU.subtract))
            settled()
            mine(dve.tensor_scalar(bonus[:], bonus[:], BONUS_LOW, None, ALU.max))
            settled()
            dve.tensor_scalar(shift[:], bonus[:], 0.0, SHIFT_LOW, ALU.min, ALU.max).then_inc(prep_rdy, 1)

            def moments(stats, mean, var):
                settled()
                mine(dve.tensor_tensor(half_diff[:], stats[:, :, 1], stats[:, :, 4], ALU.subtract))
                mine(dve.tensor_tensor(mean[:], stats[:, :, 1], stats[:, :, 4], ALU.add))
                mine(dve.tensor_tensor(var[:], stats[:, :, 2], stats[:, :, 5], ALU.add))
                settled()
                mine(dve.scalar_tensor_tensor(half_diff[:], half_diff[:], 0.25, half_diff[:], ALU.mult, ALU.mult))
                mine(dve.tensor_scalar(mean[:], mean[:], 0.5, None, ALU.mult))
                settled()
                mine(dve.scalar_tensor_tensor(var[:], var[:], 1.0 / D, half_diff[:], ALU.mult, ALU.add))
                settled()

            def norm1(n, first):
                dve.wait_ge(x_ld, 16 * (n + 1))
                for tb in range(TB):
                    op = dve.bn_stats(bn6[:, tb, :], x_sb[:, tb, :])
                mine(op)
                moments(bn6, mean, var)
                dve.tensor_scalar(var_eps[:], var[:], LN_EPS, None, ALU.add).then_inc(stats1, 1)

            def norm1_apply(n, first):
                dve.wait_ge(rstd1, n + 1)
                if not first:
                    dve.wait_ge(hnT_ps, n * DB)
                for tb in range(TB):
                    op = dve.tensor_scalar(norm[:, tb, :], x_sb[:, tb, :], mean[:, tb:tb + 1], rstd[:, tb:tb + 1],
                                           ALU.subtract, ALU.mult)
                op.then_inc(xn_rdy, 1)

            def keys(n, cb, first):
                dve.wait_ge(xnT_ps, n * DB + cb + 1)
                if cb == 0 and not first:
                    dve.wait_ge(pv_ps, n * G)
                if cb >= 2:
                    dve.wait_ge(yT_rdy, n * DB + cb - 1)
                dve.scalar_tensor_tensor(kexp[cb % 2][:], steps[:], neg_wp[:, cb:cb + 1], ps[:, TPB, :],
                                         ALU.mult, ALU.add).then_inc(kt_rdy, 1)

            def scans(n, cb):
                if cb == 0:
                    dve.memset(p_run[:, 0:1], 0.0)
                    dve.memset(q_run[:, 0:1], 0.0)
                a = decay[:, cb:cb + 1].broadcast_to([P, T])
                dve.wait_ge(kv_rdy, n * DB + cb + 1)
                dve.tensor_tensor_scan(q_run[:, 1:T + 1], a, kexp[cb % 2][:], 0.0, ALU.mult, ALU.add)
                mine(dve.tensor_tensor_scan(p_run[:, 1:T + 1], a, kv[cb % 2][:], 0.0, ALU.mult, ALU.add))
                settled()
                dve.scalar_tensor_tensor(kexp[cb % 2][:], q_run[:, 0:T], rho[:, cb:cb + 1], kexp[cb % 2][:], ALU.mult, ALU.add)
                mine(dve.scalar_tensor_tensor(kv[cb % 2][:], p_run[:, 0:T], rho[:, cb:cb + 1], kv[cb % 2][:], ALU.mult, ALU.add))

            def quotient(n, cb):
                settled()
                mine(dve.reciprocal(kexp[cb % 2][:], kexp[cb % 2][:]))
                settled()
                dve.tensor_tensor(yT[:, cb, :], kv[cb % 2][:], kexp[cb % 2][:], ALU.mult).then_inc(yT_rdy, 1)

            def residual1(n, tb):
                dve.wait_ge(yT_ps, n * TB + tb + 1)
                dve.scalar_tensor_tensor(x_sb[:, tb, :], ps[:, TPB, :], gate_t[:, 0:1], x_sb[:, tb, :],
                                         ALU.mult, ALU.add).then_inc(x1_rdy, 1)
                dve.wait_ge(x1_rdy, n * TB + tb + 1)
                mine(dve.bn_stats(bn6b[:, tb, :], x_sb[:, tb, :]))

            def norm2(n):
                moments(bn6b, meanb, varb)
                dve.tensor_scalar(var_epsb[:], varb[:], LN_EPS, None, ALU.add).then_inc(stats2, 1)
                dve.wait_ge(rstd2, n + 1)
                mine(dve.tensor_tensor(vr[:], varb[:], rstdb[:], ALU.mult))
                settled()
                mine(dve.tensor_tensor(vr[:], vr[:], rstdb[:], ALU.mult))
                settled()
                dve.tensor_scalar(ms_eps[:], vr[:], RMS_EPS, None, ALU.add).then_inc(ms2, 1)
                mine(dve.tensor_scalar(gr[:], rstdb[:], gate_t[:, 1:2], None, ALU.mult))
                settled()
                dve.tensor_scalar(base_mul[:], gr[:], 1.0, None, ALU.add)
                mine(dve.scalar_tensor_tensor(base_add[:], meanb[:], -1.0, gr[:], ALU.mult, ALU.mult))
                dve.wait_ge(rms2, n + 1)
                mine(dve.tensor_tensor(hn_scale[:], rstdb[:], rms[:], ALU.mult))
                settled()
                dve.wait_ge(xnT_ps, (n + 1) * DB)
                for tb in range(TB):
                    op = dve.tensor_scalar(norm[:, tb, :], x_sb[:, tb, :], meanb[:, tb:tb + 1], hn_scale[:, tb:tb + 1],
                                           ALU.subtract, ALU.mult)
                op.then_inc(hn_rdy, 1)

            norm1(0, True)
            norm1_apply(0, True)
            dve.wait_ge(decay_rdy, 1)
            dve.tensor_scalar(half_gate[:], gate_t[:, 1:2], 0.5, None, ALU.mult)
            dve.wait_ge(const_rdy, 5)
            for cb in range(DB):
                keys(0, cb, True)
                if cb >= 1:
                    scans(0, cb - 1)
                    quotient(0, cb - 1)
            scans(0, DB - 1)
            quotient(0, DB - 1)
            for i, (raw, dst) in enumerate(((raw_wq, wq_s), (raw_wk, wk_s))):
                for db in range(DB):
                    dve.wait_ge(wsplit_hi, DB * i + db + 1)
                    dve.scalar_tensor_tensor(dst[1][:, db, :], raw[:, db, :], ln1_sb[:, db:db + 1], f32(dst[0][:, db, :]),
                                             ALU.mult, ALU.subtract).then_inc(wsplit_lo, 1)
            dve.wait_ge(wsplit_hi, 2 * DB + 1)
            dve.tensor_tensor(b_s[4 * R:5 * R, :], raw_b[4 * R:5 * R, :], f32(b_s[4 * R:5 * R, :]), ALU.subtract).then_inc(wsplit_lo, 1)
            mine(dve.memset(woa[:], 0.0))
            dve.wait_ge(woa_ps, 1)
            settled()
            for j in range(4):
                op = dve.tensor_copy(woa[quad(j), :, R * j:R * j + R], ps[quad(j), 4, 0:DB * R].rearrange("p (t r) -> p t r", r=R))
            op.then_inc(woa_sb, 1)
            for tb in range(TB):
                residual1(0, tb)
            norm2(0)
            for db in range(DB):
                dve.wait_ge(wsplit_hi, 2 * DB + 1 + db + 1)
                if db == 0:
                    dve.wait_ge(wsplit_hi, 3 * DB + 1)
                dve.scalar_tensor_tensor(ga_s[1][:, db, 0:H * R], ps[:, 5 + db // 2, 256 * (db % 2):256 * (db % 2) + 256],
                                         ln1_sb[:, db:db + 1], f32(ga_s[0][:, db, 0:H * R]), ALU.mult, ALU.subtract)
                dve.scalar_tensor_tensor(ga_s[1][:, db, H * R:GA], a_sb[:, db, :], ln2_sb[:, db:db + 1],
                                         f32(ga_s[0][:, db, H * R:GA]), ALU.mult, ALU.subtract).then_inc(wsplit_lo, 1)
            own_prologue = own["n"]

            def low_gu(b, f):
                dve.wait_ge(gu_hi, b * NF + f + 1)
                dve.tensor_tensor(gu_s[f % 2][1][:], raw_gu[f % 2][:], f32(gu_s[f % 2][0][:]), ALU.subtract).then_inc(gu_lo, 1)

            def low_d(b, f):
                dve.wait_ge(wd_hi, b * NF + f + 1)
                dve.tensor_tensor(wd_s[f % 2][1][:], raw_d[f % 2][:], f32(wd_s[f % 2][0][:]), ALU.subtract).then_inc(wd_lo, 1)

            def finish(b):
                for tb in range(TB):
                    if tb == 0:
                        dve.wait_ge(down_ps, (b + 1) * NF)
                    if tb >= 2:
                        dve.wait_ge(out_st[tb % 2], b * 32 + 16)
                    dve.scalar_tensor_tensor(out_sb[tb % 2][:], ps[:, tb, :], half_gate[:], base[:, tb, :],
                                             ALU.mult, ALU.add).then_inc(fin_rdy, 1)
                dve.wait_ge(fin_rdy, (b + 1) * TB)

            def make_base(b):
                for tb in range(TB):
                    op = dve.tensor_scalar(base[:, tb, :], x_sb[:, tb, :], base_mul[:, tb:tb + 1], base_add[:, tb:tb + 1],
                                           ALU.mult, ALU.add)
                op.then_inc(base_rdy, 1)

            def batch(b, last):
                own["base"], own["n"] = own_prologue + b * DVE_OWN_PER_BATCH, 0
                make_base(b)
                for db in range(DB):
                    dve.wait_ge(hT_hi, b * DB + db + 1)
                    dve.tensor_tensor(hn_s[1][:, db, :], ps[:, 4 + db, :], f32(hn_s[0][:, db, :]), ALU.subtract)
                    dve.scalar_tensor_tensor(h_s[1][:, db, :], ps[:, 4 + db, :], ln2_sb[:, db:db + 1], f32(h_s[0][:, db, :]),
                                             ALU.mult, ALU.subtract).then_inc(hT_lo, 1)

                def qk_low(g):
                    for i, (st, at) in enumerate(((q_st, 32), (k_st, 64))):
                        for j in range(4):
                            dve.wait_ge(qk_hi, b * 8 * G + 8 * g + 4 * i + j + 1)
                            op = dve.tensor_tensor(st[g % 3][at:at + 32, j, :], ps[quad(j), 4 + i, :], f32(st[g % 3][0:32, j, :]),
                                                   ALU.subtract)
                        op.then_inc(qk_lo, 1)

                def maxima(g, s, pr):
                    dve.wait_ge(s_ps, b * 6 * G + 6 * g + 2 * s + pr + 1)
                    for at, qb in S_STEPS[s]:
                        op = dve.reduce_max(mx[:, qb, 2 * pr:2 * pr + 2], ps[:, 0:2, at:at + (qb + 1) * P], AX.X)
                    op.then_inc(smax_rdy, 1)

                def minus_max(g):
                    dve.wait_ge(smax_rdy, b * 6 * G + 6 * g + 6)
                    mine(dve.tensor_scalar(nmc[:, :, 0:4].bitcast(F32R), mx[:], -1.0, None, ALU.mult))
                    settled()
                    dve.scalar_tensor_tensor(nmc[:, :, 4:8], mx[:], -1.0, nmc[:, :, 0:4], ALU.mult, ALU.subtract).then_inc(nmc_rdy, 1)
                    dve.wait_ge(nm_ps, b * G + g + 1)
                    if g >= 1:
                        dve.wait_ge(nm_ld[g - 1], 32 * (b + 1))
                    dve.tensor_copy(nmrow[:], ps[0:8, TPB, :]).then_inc(nmrow_rdy, 1)

                def weighted(g):
                    dve.wait_ge(pv_ps, b * G + g + 1)
                    dve.tensor_copy(pvs[:], ps[:, 6, :]).then_inc(pvs_rdy, 1)
                    dve.wait_ge(pvT_ps, b * G + g + 1)
                    pvT = ps[:, TPB, :].rearrange("p (q j c) -> p q j c", q=TB, j=4)
                    mine(dve.reciprocal(rl[:], pvT[:, :, :, R]))
                    settled()
                    for qb in range(TB):
                        op = dve.tensor_tensor(pvn[:, qb, :, :], pvT[:, qb, :, 0:R], rl[:, qb, :].unsqueeze(2).broadcast_to([P, 4, R]), ALU.mult)
                    op.then_inc(pvT_used, 1)
                    dve.wait_ge(pvT_used, b * G + g + 1)
                    mine(dve.reduce_sum(modp[:, g, :, :], pvn[:].rearrange("p q j r -> p q r j"), AX.X))

                qk_low(0)
                qk_low(1)
                for g in range(G + 1):
                    if g < G:
                        for k in range(6):
                            maxima(g, k // 2, k % 2)
                            if k == 3 and 1 <= g and g + 1 < G:
                                qk_low(g + 1)
                        minus_max(g)
                    if g >= 1:
                        weighted(g - 1)
                settled()
                dve.reduce_sum(modsum[:], modp[:].rearrange("p g q r -> p q r g"), AX.X).then_inc(modsum_rdy, 1)
                low_gu(b, 0)
                low_gu(b, 1)
                low_d(b, 0)
                dve.wait_ge(modt_rdy, b + 1)
                mine(dve.scalar_tensor_tensor(t_mod[:], modt[:], MOD_SCALE, h_a[:], ALU.mult, ALU.mult))
                settled()
                dve.tensor_copy(tcols[:, :, 0:R].bitcast(F32R), t_mod[:])
                mine(dve.tensor_copy(tcols[:, :, 4 * R:5 * R].bitcast(F32R), t_mod[:]))
                settled()
                dve.tensor_tensor(tcols[:, :, 2 * R:3 * R], t_mod[:], tcols[:, :, 0:R], ALU.subtract).then_inc(t_rdy, 1)
                dve.wait_ge(tT_ps, b + 1)
                dve.tensor_copy(t_s[:], ps[0:5 * R, TPB, :]).then_inc(tT_rdy, 1)

                for f in range(NF):
                    dve.wait_ge(th_rdy, b * NF + f + 1)
                    if f >= 1:
                        dve.wait_ge(prod_rdy, b * NF + f)
                    mine(dve.scalar_tensor_tensor(gsil[:], th[:], 1.0, ps[:, 4 + (2 * f) % 3, :], ALU.add, ALU.mult))
                    dve.wait_ge(up_ps, b * NF + f + 1)
                    settled()
                    if f >= 1:
                        dve.wait_ge(act_lo, b * NF + f)
                    dve.tensor_tensor(prod[:], gsil[:], ps[:, 4 + (2 * f + 1) % 3, :], ALU.mult).then_inc(prod_rdy, 1)
                    dve.wait_ge(act_hi, b * NF + f + 1)
                    dve.tensor_tensor(act_s[f % 2][1][:], prod[:], f32(act_s[f % 2][0][:]), ALU.subtract).then_inc(act_lo, 1)
                    if f + 2 < NF:
                        low_gu(b, f + 2)
                    if f + 1 < NF:
                        low_d(b, f + 1)
                    if not last:
                        n = b + 1
                        if f == 0:
                            norm1(n, False)
                        if f == 1:
                            norm1_apply(n, False)
                        if f in range(2, 2 + 2 * DB, 2):
                            keys(n, f // 2 - 1, False)
                        if 3 <= f < 3 + 2 * DB:
                            (scans if f % 2 else quotient)(n, (f - 3) // 2)
                        if 11 <= f < 11 + TB:
                            residual1(n, f - 11)
                        if f == NF - 1:
                            norm2(n)
                finish(b)
                assert last or own["n"] == DVE_OWN_PER_BATCH, own["n"]

            with dve.Fori(0, NB - 1) as b:
                batch(b, False)
            batch(NB - 1, True)

        @block.tensor
        def _(pe):
            def split_matmul(dst, w_hi, w_lo, m_hi, m_lo, start, stop):
                pe.matmul(dst, w_hi, m_hi, start=start, stop=False)
                pe.matmul(dst, w_hi, m_lo, start=False, stop=False)
                return pe.matmul(dst, w_lo, m_hi, start=False, stop=stop)

            def keys_T(n, cb):
                pe.wait_ge(xn_rdy, n + 1)
                if cb >= 1:
                    pe.wait_ge(kt_rdy, n * DB + cb)
                for tb in range(TB):
                    op = pe.transpose(ps[:, TPB, blk(tb)], norm[:, tb, blk(cb)], ident[:])
                op.then_inc(xnT_ps, 1)

            def rows_y(n, tb):
                pe.wait_ge(yT_rdy, (n + 1) * DB)
                if tb >= 1:
                    pe.wait_ge(x1_rdy, n * TB + tb)
                for cb in range(DB):
                    op = pe.transpose(ps[:, TPB, blk(cb)], yT[:, cb, blk(tb)], ident[:])
                op.then_inc(yT_ps, 1)

            pe.wait_ge(const_rdy, 6)
            pe.wait_ge(woa_ld, 48)
            for jt in range(DB):
                for ot in range(DB):
                    op = pe.matmul(ps[:, 4, R * jt:R * jt + R], raw_wo[:, ot, blk(jt)], a_sb[:, ot, :],
                                   start=ot == 0, stop=ot == DB - 1)
            op.then_inc(woa_ps, 1)
            for cb in range(DB):
                keys_T(0, cb)
            pe.wait_ge(woa_sb, 1)
            for db in range(DB):
                for jt in range(DB):
                    at = 256 * (db % 2) + 4 * R * jt
                    op = pe.matmul(ps[:, 5 + db // 2, at:at + 4 * R], raw_wv[:, jt, blk(db)], woa[:, jt, :], start=True, stop=True)
            op.then_inc(ga_ps, 1)
            for tb in range(TB):
                rows_y(0, tb)
            pe.wait_ge(wsplit_lo, 3 * DB + 1)
            pe.wait_ge(ones_rdy, 3)
            pe.wait_ge(const_rdy, 8)

            def batch(b, last):
                pe.wait_ge(hn_rdy, b + 1)
                for db in range(DB):
                    for tb in range(TB):
                        op = pe.transpose(ps[:, 4 + db, blk(tb)], norm[:, tb, blk(db)], ident[:])
                    op.then_inc(hnT_ps, 1)

                def project(g, i):
                    w = (wq_s, wk_s)[i]
                    if g >= 1:
                        pe.wait_ge(qk_lo, b * 2 * G + 2 * (g - 1) + i + 1)
                    for db in range(DB):
                        op = split_matmul(ps[:, 4 + i, :], w[0][:, db, blk(g)], w[1][:, db, blk(g)], hn_s[0][:, db, :], hn_s[1][:, db, :],
                                          db == 0, db == DB - 1)
                    op.then_inc(qk_ps, 1)

                def values(tb):
                    if tb >= 2:
                        pe.wait_ge(va_sb, b * TB + tb - 1)
                    for db in range(DB):
                        op = split_matmul(ps[:, 6 + tb % 2, 0:GA], hn_s[0][:, db, blk(tb)], hn_s[1][:, db, blk(tb)],
                                          ga_s[0][:, db, :], ga_s[1][:, db, :], db == 0, db == DB - 1)
                    op.then_inc(va_ps, 1)

                def scores(g, k):
                    s, pr = k // 2, k % 2
                    if k == 0:
                        pe.wait_ge(rep_ld[g], 32 * (b + 1))
                        pe.wait_ge(qk_lo, b * 2 * G + 2 * g + 2)
                    if g == 0 and k == 0:
                        pe.wait_ge(base_rdy, b + 1)
                    else:
                        pe.wait_ge(smax_rdy, b * 6 * G + 6 * g + k)
                    for i in range(2):
                        j = 2 * pr + i
                        for at, qb in S_STEPS[s]:
                            n = (qb + 1) * P
                            pe.matmul(ps[:, i, at:at + n], q_st[g % 3][0:96, j, blk(qb)], k_st[g % 3][0:96, j, 0:n], start=True, stop=False)
                            op = pe.matmul(ps[:, i, at + n - P:at + n], identb[:], mask_qk[:], start=False, stop=True)
                    op.then_inc(s_ps, 1)

                def scores_T(g, k):
                    s, pr = k // 2, k % 2
                    if k == 0:
                        pe.wait_ge(nm_ld[g], 32 * (b + 1))
                    if g > 0 or k > 0:
                        pe.wait_ge(exp_rdy, b * 6 * G + 6 * g + k)
                    for i in range(2):
                        j = 2 * pr + i
                        for at, kb in ST_STEPS[s]:
                            n = T - kb * P
                            pe.matmul(ps[:, 2 + i, at:at + n], k_st[g % 3][0:98, j, blk(kb)], q_st[g % 3][0:98, j, kb * P:T], start=True, stop=False)
                            op = pe.matmul(ps[:, 2 + i, at:at + P], identb[:], mask_kq[:], start=False, stop=True)
                    op.then_inc(st_ps, 1)

                def maxima_T(g):
                    pe.wait_ge(nmc_rdy, b * G + g + 1)
                    if g == 0:
                        pe.wait_ge(va_sb, (b + 1) * TB)
                    elif g >= 2:
                        pe.wait_ge(pvT_used, b * G + g - 1)
                    for qb in range(TB):
                        op = pe.transpose(ps[0:8, TPB, blk(qb)], nmc[:, qb, :], ident[:])
                    op.then_inc(nm_ps, 1)

                def weigh(g):
                    pe.wait_ge(exp_rdy, b * 6 * G + 6 * g + 6)
                    if g >= 1:
                        pe.wait_ge(pvs_rdy, b * G + g)
                    for kb in range(TB):
                        n = T - kb * P
                        for j in range(4):
                            op = pe.matmul(ps[quad(j), 6, kb * P:T], v_aug[:, kb, 4 * g + j, :], e_row[:, j, E_AT[kb]:E_AT[kb] + n],
                                           start=kb == 0, stop=kb == TB - 1)
                    op.then_inc(pv_ps, 1)

                def weighed_T(g):
                    pe.wait_ge(pvs_rdy, b * G + g + 1)
                    pe.wait_ge(nmrow_rdy, b * G + min(g + 2, G))
                    for qb in range(TB):
                        op = pe.transpose(ps[:, TPB, blk(qb)], pvs[:, blk(qb)], ident[:])
                    op.then_inc(pvT_ps, 1)

                pe.wait_ge(hT_lo, (b + 1) * DB)
                project(0, 0)
                project(0, 1)
                for tb in range(TB):
                    values(tb)
                project(1, 0)
                project(1, 1)
                for g in range(G + 1):
                    for k in range(6):
                        if g < G:
                            scores(g, k)
                        if g >= 1:
                            scores_T(g - 1, k)
                        if 1 <= g and g + 1 < G and k in (1, 3):
                            project(g + 1, k // 2)
                    if g < G:
                        maxima_T(g)
                    if g >= 1:
                        weigh(g - 1)
                        weighed_T(g - 1)

                def gate(f):
                    if f == 0:
                        pe.wait_ge(qk_lo, (b + 1) * 2 * G)
                    elif f >= 2:
                        pe.wait_ge(prod_rdy, b * NF + f - 1)
                    pe.wait_ge(gu_lo, b * NF + f + 1)
                    for db in range(DB):
                        split_matmul(ps[:, 4 + (2 * f) % 3, :], gu_s[f % 2][0][:, blk(db)], gu_s[f % 2][1][:, blk(db)],
                                     h_s[0][:, db, :], h_s[1][:, db, :], db == 0, False)

                def gate_mod(f):
                    if f == 0:
                        pe.wait_ge(tT_rdy, b + 1)
                    pe.matmul(ps[:, 4 + (2 * f) % 3, :], b_s[:, blk(f)], t_s[:], start=False, stop=True).then_inc(gate_ps, 1)

                def up(f):
                    if f >= 1:
                        pe.wait_ge(prod_rdy, b * NF + f)
                    for db in range(DB):
                        op = split_matmul(ps[:, 4 + (2 * f + 1) % 3, :], gu_s[f % 2][0][:, D + db * P:D + (db + 1) * P],
                                          gu_s[f % 2][1][:, D + db * P:D + (db + 1) * P],
                                          h_s[0][:, db, :], h_s[1][:, db, :], db == 0, db == DB - 1)
                    op.then_inc(up_ps, 1)

                def down(f):
                    pe.wait_ge(act_lo, b * NF + f + 1)
                    pe.wait_ge(wd_lo, b * NF + f + 1)
                    for tb in range(TB):
                        op = split_matmul(ps[:, tb, :], act_s[f % 2][0][:, blk(tb)], act_s[f % 2][1][:, blk(tb)],
                                          wd_s[f % 2][0][:], wd_s[f % 2][1][:], f == 0, f == NF - 1)
                    op.then_inc(down_ps, 1)

                for f in range(NF):
                    gate(f)
                    if f > 0:
                        gate_mod(f)
                    up(f)
                    if f == 0:
                        pe.wait_ge(t_rdy, b + 1)
                        pe.wait_ge(pvT_used, (b + 1) * G)
                        for tb in range(TB):
                            op = pe.transpose(ps[0:5 * R, TPB, blk(tb)], tcols[:, tb, :], ident[:])
                        op.then_inc(tT_ps, 1)
                        gate_mod(0)
                    if not last:
                        if f in range(2, 2 + 2 * DB, 2):
                            keys_T(b + 1, f // 2 - 1)
                        if 11 <= f < 11 + TB:
                            rows_y(b + 1, f - 11)
                    if f >= 1:
                        down(f - 1)
                down(NF - 1)

            with pe.Fori(0, NB - 1) as b:
                batch(b, False)
            batch(NB - 1, True)


def kernel(x, ctx_2048, g_xattn, g_ffn, L0_xattn_w, L0_xattn_u, L0_ffn_ln1_w, L0_ffn_ln2_w, L0_ffn_Wq, L0_ffn_Wk,
           L0_ffn_Wv, L0_ffn_Wo, L0_ffn_A, L0_ffn_B, L0_ffn_W_in_base, L0_ffn_W_up_base, L0_ffn_W_down):
    from concourse import bacc
    from concourse.bass_utils import run_bass_kernel_spmd

    a = np.asarray
    col = lambda v: np.ascontiguousarray(a(v).reshape(DB, P).T)
    tiles = lambda m: a(m).reshape(NF, P, DB, P).transpose(0, 3, 2, 1)
    w_gu = np.ascontiguousarray(np.stack([tiles(L0_ffn_W_in_base), tiles(L0_ffn_W_up_base)], axis=2).reshape(NF, P, 2 * D))
    arrays = {
        "x": a(x),
        "ctxT": np.ascontiguousarray(a(ctx_2048).transpose(0, 2, 1)),
        "w4": col(L0_xattn_w), "u4": col(L0_xattn_u),
        "gates": np.ascontiguousarray(np.broadcast_to(np.concatenate([a(g_xattn), a(g_ffn)])[None, :], (P, 2))),
        "ln1": col(L0_ffn_ln1_w), "ln2": col(L0_ffn_ln2_w),
        "wqT": np.ascontiguousarray(a(L0_ffn_Wq).T), "wkT": np.ascontiguousarray(a(L0_ffn_Wk).T),
        "wv": a(L0_ffn_Wv), "wo": a(L0_ffn_Wo), "a4": a(L0_ffn_A), "b_mod": a(L0_ffn_B),
        "w_gu": w_gu, "w_down": np.ascontiguousarray(a(L0_ffn_W_down).T),
    }
    arrays = {f"{k}_dram": np.ascontiguousarray(v) for k, v in arrays.items()}
    nc = bacc.Bacc("TRN2", target_bir_lowering=False, num_devices=1, dynamic_dma_scratch_size=DGE_SCRATCH)
    args = [nc.dram_tensor(k, v.shape, F32, kind="ExternalInput").ap() for k, v in arrays.items()]
    args.append(nc.dram_tensor("out_dram", (NB, T, D), F32, kind="ExternalOutput").ap())
    flamingo_layer(nc, *args)
    return run_bass_kernel_spmd(nc, [arrays], core_ids=[0]).results[0]["out_dram"]
```

```python
from contextlib import ExitStack

import numpy as np

import concourse.bass as bass
import concourse.mybir as mybir

F32, F32R, BF16 = mybir.dt.float32, mybir.dt.float32r, mybir.dt.bfloat16
ALU, ACT, AX = mybir.AluOpType, mybir.ActivationFunctionType, mybir.AxisListType

NB, T, D = 4, 512, 512
FF, R, H = 2048, 16, 16
HD = D // H
P = 128
TB, DB = T // P, D // P
NF = FF // P
G = H // 4
VW = 32
GA = H * R + R
LN_EPS, RMS_EPS = 1e-5, 1e-6
MASKED = -1e30
SM_SCALE = float(1.0 / np.sqrt(np.float32(HD)))
MOD_SCALE = 0.1
BONUS_LOW, SHIFT_LOW = -70.0, -40.0
DGE_SCRATCH = 1024
DVE_OWN_PER_BATCH = 46

E_AT = [0, 640, 1024, 512]
S_STEPS = [[(0, 3)], [(P, 2), (0, 0)], [(0, 1)]]
ST_STEPS = [[(0, 0)], [(P, 1), (0, 3)], [(0, 2)]]
ST_E = [(0, 512), (512, 512), (1024, 256)]

STEPS = 6 * G
LAG = 8
PROJ_AT = {1: -2, 2: 3, 3: 10}
ROUND_AT = {0: (1, 0), 2: (1, 1), 5: (2, 0), 7: (2, 1), 13: (3, 0), 14: (3, 1)}
LOW_AT = {0: [(1, 0, 0)], 1: [(1, 0, 2)], 2: [(1, 1, 0)], 3: [(1, 1, 2)], 5: [(2, 0, 0)], 6: [(2, 0, 2)], 7: [(2, 1, 0)], 8: [(2, 1, 2)], 14: [(3, 0, 0)], 15: [(3, 0, 2), (3, 1, 0)], 16: [(3, 1, 2)]}
NORM_LAG = LAG + 8
BASE_AT = 4
TWO_PAIRS = 17
VALUE_BANK = [6, 7, 7, 6]
VALUE_AT = {2: 2, 3: 3}
HB = [6, 7, 4, 5]
H_ORDER = [2, 3, 0, 1]
st_bank = lambda m: 0 if m >= TWO_PAIRS and m % 2 else 2
KEYS_AT, SCANS_AT, RECIP_AT = [2, 3, 5, 6], [3, 4, 6, 7], [(3, 4), (5, 5), (6, 7), (8, 8)]
Y_AT, NORM2_AT = 9, 13


def flamingo_layer(nc, x, ctxT, w4, u4, gates, ln1, ln2, wqT, wkT, wv, wo, a4, b_mod, w_gu, w_down, out):
    es = ExitStack()
    with es:
        top = [nc.sbuf_base + (-nc.sbuf_base) % 64]

        def place(name, shape, dt, at=None):
            size = int(np.prod(shape[1:])) * (2 if dt == BF16 else 4)
            size += -size % 64
            off = top[0] if at is None else at[0]
            if at is None:
                top[0] += size
            else:
                at[0] += size
                assert at[0] <= at[1], name
            return nc.alloc_sbuf_tensor_at(name, shape, dt, offset=off)

        def region(size):
            at = top[0]
            top[0] += size
            return [at, at + size]

        def sem(name):
            return es.enter_context(nc.semaphore(name))

        ident = place("ident", [P, P], F32)
        identb = place("identb", [P, P], BF16)
        mask_qk = place("mask_qk", [P, P], BF16)
        mask_kq = place("mask_kq", [P, P], BF16)
        steps = place("steps", [P, T], F32)
        w_sb = place("w_sb", [P, DB], F32)
        u_sb = place("u_sb", [P, DB], F32)
        gates_sb = place("gates_sb", [P, 2], F32)
        ln1_sb = place("ln1_sb", [P, DB], F32)
        ln2_sb = place("ln2_sb", [P, DB], F32)
        a_sb = place("a_sb", [P, DB, R], F32)
        neg_wp = place("neg_wp", [P, DB], F32)
        w_minus = place("w_minus", [P, DB], F32)
        decay = place("decay", [P, DB], F32)
        bonus = place("bonus", [P, DB], F32)
        shift = place("shift", [P, DB], F32)
        rho = place("rho", [P, DB], F32)
        gate_t = place("gate_t", [P, 2], F32)
        half_gate = place("half_gate", [P, 1], F32)
        minus_half = place("minus_half", [P, TB], F32)
        wq_s = [place(f"wq_{n}", [P, DB, D], F32R) for n in ("hi", "lo")]
        wk_s = [place(f"wk_{n}", [P, DB, D], F32R) for n in ("hi", "lo")]
        ga_s = [place(f"ga_{n}", [P, DB, GA], F32R) for n in ("hi", "lo")]
        b_s = place("b_s", [5 * R, FF], F32R)
        v_aug = place("v_aug", [P, TB, H, VW], F32)
        k_st = [place(f"k_st{i}", [P, 4, T], F32R) for i in range(3)]
        base_at = region(8192)
        raw_b = place("raw_b", [5 * R, FF], F32, list(base_at))
        base = place("base", [P, TB, D], F32, base_at)
        h_at = region(16384)
        first_at = list(h_at)
        h_s = [place(f"h_{n}", [P, DB, T], F32R, h_at) for n in ("hi", "lo")]
        raw_gu = [place(f"raw_gu{i}", [P, 2 * D], F32) for i in range(2)]
        raw_d = [place(f"raw_d{i}", [P, D], F32) for i in range(2)]
        bn6 = place("bn6", [P, TB, 6], F32)
        mean = place("mean", [P, TB], F32)
        var = place("var", [P, TB], F32)
        half_diff = place("half_diff", [P, TB], F32)
        var_eps = place("var_eps", [P, TB], F32)
        rstd = place("rstd", [P, TB], F32)
        bn6b = place("bn6b", [P, TB, 6], F32)
        meanb = place("meanb", [P, TB], F32)
        varb = place("varb", [P, TB], F32)
        var_epsb = place("var_epsb", [P, TB], F32)
        rstdb = place("rstdb", [P, TB], F32)
        vr = place("vr", [P, TB], F32)
        ms_eps = place("ms_eps", [P, TB], F32)
        rms = place("rms", [P, TB], F32)
        hn_scale = place("hn_scale", [P, TB], F32)
        gr = place("gr", [P, TB], F32)
        base_mul = place("base_mul", [P, TB], F32)
        base_add = place("base_add", [P, TB], F32)
        mx = place("mx", [P, TB, 4], F32)
        nmc = place("nmc", [P, TB, 8], F32)
        nmrow = place("nmrow", [8, T], F32R)
        pvs = place("pvs", [P, T], F32)
        rl = place("rl", [P, TB, 4], F32)
        pvn = place("pvn", [P, TB, 4, R], F32)
        modp = place("modp", [P, G, TB, R], F32)
        modsum = place("modsum", [P, TB, R], F32)
        modt = place("modt", [P, TB, R], F32)
        h_a = place("h_a", [P, TB, R], F32)
        t_mod = place("t_mod", [P, TB, R], F32)
        tcols = place("tcols", [P, TB, 5 * R], F32)
        t_s = place("t_s", [5 * R, T], F32R)

        wide = region(24576 + 2 * 8192)
        e_at = [wide[0] + 16384, wide[1]]
        r2 = [wide[0], wide[0] + 24576]
        norm_at = [r2[1], r2[1] + 8192]
        x_at = [norm_at[1], norm_at[1] + 8192]
        norm = place("norm", [P, TB, D], F32, norm_at)
        x_sb = place("x_sb", [P, TB, D], F32, x_at)
        r2a, r2s = list(r2), list(r2)
        hn_s = [place(f"hn_{n}", [P, DB, T], F32R, r2a) for n in ("hi", "lo")]
        raw_wq = place("raw_wq", [P, DB, D], F32, r2s)
        raw_wk = place("raw_wk", [P, DB, D], F32, r2s)
        raw_wv = place("raw_wv", [P, DB, D], F32, r2s)
        gu_s = [[place(f"gu{i}_{n}", [P, 2 * D], F32R, r2) for n in ("hi", "lo")] for i in range(2)]
        wd_s = [[place(f"wd{i}_{n}", [P, D], F32R, r2) for n in ("hi", "lo")] for i in range(2)]
        r1 = region(45056)
        r1a = list(r1)
        q_st = [place(f"q_st{i}", [P, 4, T], F32R, r1a) for i in range(3)]
        e_row = [place("e_row0", [P, 4, 1280], F32, r1a), place("e_row1", [P, 4, 1280], F32, e_at)]
        vT = place("vT", [P, DB, T], F32, r1)
        kexp = [place(f"kexp{i}", [P, T], F32, r1 if i < 2 else first_at) for i in range(4)]
        kv = [place(f"kv{i}", [P, T], F32, r1 if i < 2 else first_at) for i in range(4)]
        p_run = place("p_run", [P, T + 1], F32, r1)
        q_run = place("q_run", [P, T + 1], F32, r1)
        yT = place("yT", [P, DB, T], F32, r1)
        r1s = list(r1)
        raw_wo = place("raw_wo", [P, DB, D], F32, r1s)
        woa = place("woa", [P, DB, 4 * R], F32, r1s)
        th = place("th", [P, T], F32, r1)
        gsil = place("gsil", [P, T], F32, r1)
        prod = place("prod", [P, T], F32, r1)
        act_s = [[place(f"act{i}_{n}", [P, T], F32R, r1) for n in ("hi", "lo")] for i in range(2)]
        assert top[0] <= nc.sbuf_usable_end, (top[0], nc.sbuf_usable_end)

        ps = es.enter_context(nc.psum_tensor("ps", [P, 8, 512], F32))
        TPB = 7

        w_ld, woa_ld, b_ld = sem("w_ld"), sem("woa_ld"), sem("b_ld")
        small_ld, x_ld, v_ld = sem("small_ld"), sem("x_ld"), sem("v_ld")
        gu_ld = [sem(f"gu_ld{i}") for i in range(2)]
        d_ld = [sem(f"d_ld{i}") for i in range(2)]
        rep_ld = [sem(f"rep_ld{i}") for i in range(G)]
        nm_ld = [sem(f"nm_ld{i}") for i in range(G)]
        base_free = sem("base_free")
        const_rdy, prep_rdy, pool_own = sem("const_rdy"), sem("prep_rdy"), sem("pool_own")
        decay_rdy, ones_rdy = sem("decay_rdy"), sem("ones_rdy")
        woa_ps, ga_ps, woa_sb, wscaled, wsplit_hi, wsplit_lo, ga_hi, ga_lo = (sem(n) for n in (
            "woa_ps", "ga_ps", "woa_sb", "wscaled", "wsplit_hi", "wsplit_lo", "ga_hi", "ga_lo"))
        stats1, rstd1, xn_rdy, xnT_ps, kt_rdy, kexp_rdy, kv_rdy, recip_rdy, yT_rdy, yT_ps, x1_rdy = (sem(n) for n in (
            "stats1", "rstd1", "xn_rdy", "xnT_ps", "kt_rdy", "kexp_rdy", "kv_rdy", "recip_rdy", "yT_rdy", "yT_ps", "x1_rdy"))
        stats2, rstd2, ms2, rms2, hn_rdy, base_rdy, hnT_ps, hn_hi, hn_lo, h_hi, h_lo = (sem(n) for n in (
            "stats2", "rstd2", "ms2", "rms2", "hn_rdy", "base_rdy", "hnT_ps", "hn_hi", "hn_lo", "h_hi", "h_lo"))
        qk_ps, qk_hi, qk_lo, va_ps, va_sb, s_ps, smax_rdy, nmc_rdy, nm_ps, nmrow_rdy = (sem(n) for n in (
            "qk_ps", "qk_hi", "qk_lo", "va_ps", "va_sb", "s_ps", "smax_rdy", "nmc_rdy", "nm_ps", "nmrow_rdy"))
        st_ps, exp_rdy, pv_ps, pvs_rdy, pvT_ps, pvT_used, modsum_rdy, modt_rdy, t_rdy, tT_ps, tT_rdy = (sem(n) for n in (
            "st_ps", "exp_rdy", "pv_ps", "pvs_rdy", "pvT_ps", "pvT_used", "modsum_rdy", "modt_rdy", "t_rdy", "tT_ps", "tT_rdy"))
        gu_hi, gu_lo, wd_hi, wd_lo, gate_ps, up_ps, down_ps, th_rdy, gsil_rdy, prod_rdy, act_hi, act_lo, mlp_ps, fin_rdy = (sem(n) for n in (
            "gu_hi", "gu_lo", "wd_hi", "wd_lo", "gate_ps", "up_ps", "down_ps", "th_rdy", "gsil_rdy", "prod_rdy", "act_hi", "act_lo", "mlp_ps", "fin_rdy"))
        dve_own = sem("dve_own")

        f32 = lambda ap: ap.bitcast(F32)
        blk = lambda i: slice(i * P, (i + 1) * P)
        quad = lambda j: slice(32 * j, 32 * j + 32)

        k_of = lambda cb, first: kexp[cb if first else cb % 2][:]
        kv_of = lambda cb, first: kv[cb if first else cb % 2][:]

        block = es.enter_context(nc.Block())

        @block.sync
        def _(sp):
            def load_x(n):
                sp.dma_start(x_sb[:], x[bass.ds(n, 1), :, :].rearrange("o (tb p) d -> p (o tb) d", p=P)).then_inc(x_ld, 16)

            def load_v(n):
                sp.dma_start(vT[:], ctxT[bass.ds(n, 1), :, :].rearrange("o (cb p) t -> p (o cb) t", p=P)).then_inc(v_ld, 16)

            def load_gu(f):
                sp.dma_start(raw_gu[f % 2][:], w_gu[f]).then_inc(gu_ld[f % 2], 16)

            def load_d(f):
                sp.dma_start(raw_d[f % 2][:], w_down[blk(f), :]).then_inc(d_ld[f % 2], 16)

            load_x(0)
            for dst, src in ((w_sb, w4), (u_sb, u4), (gates_sb, gates), (ln1_sb, ln1), (ln2_sb, ln2)):
                sp.dma_start(dst[:], src).then_inc(small_ld, 16)
            load_v(0)
            sp.dma_start(raw_wo[:], wo.rearrange("(ot p) j -> p ot j", p=P)).then_inc(woa_ld, 16)
            sp.dma_start(a_sb[:], a4.rearrange("(ot p) r -> p ot r", p=P)).then_inc(woa_ld, 16)
            sp.dma_start(raw_wv[:], wv.rearrange("(jt p) d -> p jt d", p=P)).then_inc(woa_ld, 16)
            sp.dma_start(raw_wq[:], wqT.rearrange("(db p) j -> p db j", p=P)).then_inc(w_ld, 16)
            sp.dma_start(raw_wk[:], wkT.rearrange("(db p) j -> p db j", p=P)).then_inc(w_ld, 16)
            sp.wait_ge(const_rdy, 2)
            for row in (0, 2 * R, 4 * R):
                sp.dma_start(raw_b[row:row + R, :], b_mod).then_inc(b_ld, 16)
            for f in range(2):
                load_gu(f)
                load_d(f)

            def batch(b, last):
                def replicate(g):
                    sp.wait_ge(qk_hi, b * 8 * G + 8 * g + 4)
                    sp.dma_start(f32(q_st[g % 3][64:96, :, :]), f32(q_st[g % 3][0:32, :, :])).then_inc(rep_ld[g], 16)
                    sp.wait_ge(qk_hi, b * 8 * G + 8 * g + 8)
                    sp.dma_start(f32(k_st[g % 3][32:64, :, :]), f32(k_st[g % 3][0:32, :, :])).then_inc(rep_ld[g], 16)

                def maxima(g):
                    sp.wait_ge(nmrow_rdy, b * G + g + 1)
                    for c in range(2):
                        sp.dma_start(f32(q_st[g % 3][96 + c:97 + c, :, :]), f32(nmrow[4 * c:4 * c + 4, :])).then_inc(nm_ld[g], 16)

                replicate(0)
                replicate(1)
                maxima(0)
                replicate(2)
                maxima(1)
                replicate(3)
                maxima(2)
                maxima(3)
                if not last:
                    sp.wait_ge(pv_ps, (b + 1) * G)
                    load_x(b + 1)
                for f in (2, 3):
                    sp.wait_ge(gu_lo, b * NF + f - 1)
                    load_gu(f)
                sp.wait_ge(wd_lo, b * NF + 1)
                load_d(2)
                if not last:
                    load_v(b + 1)
                for f in range(NF):
                    if f + 4 < NF + 2 and not (last and f + 4 >= NF):
                        sp.wait_ge(gu_lo, b * NF + f + 3)
                        load_gu((f + 4) % NF)
                    if f + 3 < NF + 2 and not (last and f + 3 >= NF):
                        sp.wait_ge(wd_lo, b * NF + f + 2)
                        load_d((f + 3) % NF)
                for tb in range(TB):
                    sp.wait_ge(fin_rdy, b * TB + tb + 1)
                    sp.dma_start(out[bass.ds(b, 1), blk(tb), :].rearrange("o p d -> (o p) d"), base[:, tb, :]).then_inc(base_free, 16)

            with sp.Fori(0, NB - 1) as b:
                batch(b, False)
            batch(NB - 1, True)
            sp.wait_ge(base_free, 64 * (NB + 1))

        @block.gpsimd
        def _(pool):
            pool.memset(b_clear := f32(raw_b[:]), 0.0).then_inc(const_rdy, 1)
            pool.memset(ident[:], 0.0).then_inc(pool_own, 1)
            pool.memset(mask_qk[:], 0.0).then_inc(pool_own, 1)
            pool.memset(mask_kq[:], 0.0).then_inc(pool_own, 1)
            pool.memset(minus_half[:], -0.5).then_inc(const_rdy, 1)
            pool.wait_ge(pool_own, 3)
            pool.affine_select(out=ident[:], in_=ident[:], compare_op=ALU.not_equal, fill=1.0, base=0,
                               pattern=[[-1, P]], channel_multiplier=1).then_inc(pool_own, 1)
            pool.affine_select(out=mask_qk[:], in_=mask_qk[:], compare_op=ALU.is_ge, fill=MASKED, base=0,
                               pattern=[[-1, P]], channel_multiplier=1).then_inc(const_rdy, 1)
            pool.affine_select(out=mask_kq[:], in_=mask_kq[:], compare_op=ALU.is_ge, fill=MASKED, base=0,
                               pattern=[[1, P]], channel_multiplier=-1).then_inc(const_rdy, 1)
            pool.iota(steps[:], [[1, T]], base=0, channel_multiplier=0,
                      allow_small_or_imprecise_dtypes=True).then_inc(const_rdy, 1)
            pool.wait_ge(pool_own, 4)
            pool.tensor_copy(identb[:], ident[:]).then_inc(const_rdy, 1)
            pool.memset(v_aug[:], 0.0).then_inc(pool_own, 1)
            pool.wait_ge(pool_own, 5)
            pool.memset(v_aug[:, :, :, R:R + 1], 1.0).then_inc(const_rdy, 1)
            pool.memset(tcols[:], 0.0).then_inc(const_rdy, 1)

            def rstd_of_x(n):
                pool.wait_ge(stats1, n + 1)
                pool.tensor_tensor(rstd[:], var_eps[:], minus_half[:], ALU.pow).then_inc(rstd1, 1)

            def weigh_values(n, cb, first=False):
                if cb == 0:
                    pool.wait_ge(v_ld, 16 * (n + 1))
                pool.wait_ge(kexp_rdy, n * DB + cb + 1)
                pool.tensor_tensor(kv_of(cb, first), k_of(cb, first), vT[:, cb, :], ALU.mult).then_inc(kv_rdy, 1)

            def product(n, cb, first=False):
                pool.wait_ge(recip_rdy, n * DB + cb + 1)
                pool.tensor_tensor(yT[:, cb, :], kv_of(cb, first), k_of(cb, first), ALU.mult).then_inc(yT_rdy, 1)

            def scales_of_x1(n):
                pool.wait_ge(stats2, n + 1)
                pool.tensor_tensor(rstdb[:], var_epsb[:], minus_half[:], ALU.pow).then_inc(rstd2, 1)
                pool.wait_ge(ms2, n + 1)
                pool.tensor_tensor(rms[:], ms_eps[:], minus_half[:], ALU.pow).then_inc(rms2, 1)

            def low_gu(b, f):
                pool.wait_ge(gu_hi, b * NF + f + 1)
                pool.tensor_tensor(gu_s[f % 2][1][:], raw_gu[f % 2][:], f32(gu_s[f % 2][0][:]), ALU.subtract).then_inc(gu_lo, 1)

            def low_d(b, f):
                pool.wait_ge(wd_hi, b * NF + f + 1)
                pool.tensor_tensor(wd_s[f % 2][1][:], raw_d[f % 2][:], f32(wd_s[f % 2][0][:]), ALU.subtract).then_inc(wd_lo, 1)

            rstd_of_x(0)
            pool.wait_ge(rstd1, 1)
            for i in range(3):
                pool.memset(f32(k_st[i][96:98, :, :]), 1.0).then_inc(ones_rdy, 1)
            pool.wait_ge(ones_rdy, 3)
            for cb in range(DB):
                weigh_values(0, cb, True)
            for cb in range(DB):
                for i, (raw, dst) in enumerate(((raw_wq, wq_s), (raw_wk, wk_s))):
                    pool.wait_ge(wsplit_hi, DB * i + cb + 1)
                    pool.tensor_tensor(dst[1][:, cb, :], raw[:, cb, :], f32(dst[0][:, cb, :]), ALU.subtract).then_inc(wsplit_lo, 1)
                product(0, cb, True)
            scales_of_x1(0)
            pool.wait_ge(wsplit_hi, 2 * DB + 1)
            pool.wait_ge(rms2, 1)
            pool.tensor_tensor(b_s[4 * R:5 * R, :], raw_b[4 * R:5 * R, :], f32(b_s[4 * R:5 * R, :]), ALU.subtract).then_inc(base_free, 64)
            pool.wait_ge(base_free, 64)

            def batch(b, last):
                low_gu(b, 0)
                low_gu(b, 1)
                low_d(b, 0)
                for f in range(NF):
                    if f + 2 < NF:
                        low_gu(b, f + 2)
                    if f + 1 < NF:
                        low_d(b, f + 1)
                    if not last:
                        if f == 0:
                            rstd_of_x(b + 1)
                        for cb in range(DB):
                            if f == KEYS_AT[cb]:
                                weigh_values(b + 1, cb)
                            if f == RECIP_AT[cb][1]:
                                product(b + 1, cb)
                        if f == NORM2_AT:
                            scales_of_x1(b + 1)

            with pool.Fori(0, NB - 1) as b:
                batch(b, False)
            batch(NB - 1, True)

        @block.scalar
        def _(act):
            act.wait_ge(prep_rdy, 1)
            act.activation(decay[:], w_minus[:], ACT.Exp)
            act.activation(rho[:], bonus[:], ACT.Exp, scale=-1.0)
            act.activation(gate_t[:], gates_sb[:], ACT.Tanh).then_inc(decay_rdy, 1)

            def kexp_step(n, cb, first=False):
                act.wait_ge(kt_rdy, n * DB + cb + 1)
                act.activation(k_of(cb, first), k_of(cb, first), ACT.Exp, bias=shift[:, cb:cb + 1]).then_inc(kexp_rdy, 1)

            for cb in range(DB):
                kexp_step(0, cb, True)
            act.wait_ge(w_ld, 32)
            for raw in (raw_wq, raw_wk):
                for db in range(DB):
                    act.activation(raw[:, db, :], raw[:, db, :], ACT.Copy, scale=ln1_sb[:, db:db + 1]).then_inc(wscaled, 1)
            for i, (raw, dst) in enumerate(((raw_wq, wq_s), (raw_wk, wk_s))):
                for db in range(DB):
                    act.wait_ge(wscaled, DB * i + db + 1)
                    act.activation(dst[0][:, db, :], raw[:, db, :], ACT.Copy).then_inc(wsplit_hi, 1)
            act.wait_ge(b_ld, 48)
            act.activation(b_s[:], raw_b[:], ACT.Copy).then_inc(wsplit_hi, 1)
            act.wait_ge(ga_ps, 1)
            for db in range(DB):
                act.activation(ga_s[0][:, db, 0:H * R], ps[:, 2 + db // 2, 256 * (db % 2):256 * (db % 2) + 256], ACT.Copy,
                               scale=ln1_sb[:, db:db + 1])
                act.activation(ga_s[0][:, db, H * R:GA], a_sb[:, db, :], ACT.Copy, scale=ln2_sb[:, db:db + 1]).then_inc(ga_hi, 1)

            def normed(n):
                for db in range(DB):
                    act.wait_ge(hnT_ps, n * DB + db + 1)
                    act.activation(hn_s[0][:, db, :], ps[:, HB[db], :], ACT.Copy).then_inc(hn_hi, 1)
                for db in H_ORDER:
                    act.wait_ge(hn_lo, n * DB + db + 1)
                    act.activation(h_s[0][:, db, :], ps[:, HB[db], :], ACT.Copy, scale=ln2_sb[:, db:db + 1]).then_inc(h_hi, 1)

            normed(0)

            def split_gu(b, f):
                act.wait_ge(gu_ld[f % 2], (b * NF + f - f % 2) * 8 + 16)
                if f >= 2:
                    act.wait_ge(up_ps, b * NF + f - 1)
                act.activation(gu_s[f % 2][0][:], raw_gu[f % 2][:], ACT.Copy).then_inc(gu_hi, 1)

            def split_d(b, f):
                act.wait_ge(d_ld[f % 2], (b * NF + f - f % 2) * 8 + 16)
                if f >= 2:
                    act.wait_ge(down_ps, b * (NF - 1) + f - 1)
                act.activation(wd_s[f % 2][0][:], raw_d[f % 2][:], ACT.Copy).then_inc(wd_hi, 1)

            def batch(b, last):
                def qk_round(g, i):
                    act.wait_ge(qk_ps, b * 2 * G + 2 * g + i + 1)
                    if g >= 3 and i == 0:
                        act.wait_ge(st_ps, b * STEPS + 6 * (g - 2))
                    for j in range(4):
                        act.activation((q_st, k_st)[i][g % 3][0:32, j, :], ps[quad(j), 4 + i, :], ACT.Copy).then_inc(qk_hi, 1)

                def values(tb):
                    act.wait_ge(va_ps, b * TB + tb + 1)
                    bank = VALUE_BANK[tb]
                    act.activation(v_aug[:, tb, :, 0:R], ps[:, bank, 0:H * R].rearrange("p (h r) -> p h r", r=R), ACT.Copy)
                    act.activation(h_a[:, tb, :], ps[:, bank, H * R:GA], ACT.Copy).then_inc(va_sb, 1)

                def exps(m):
                    g, s, pr = m // 6, m % 6 // 2, m % 2
                    act.wait_ge(st_ps, b * STEPS + m + 1)
                    if m == 6:
                        act.wait_ge(base_rdy, b + 1)
                    if m % 6 == 0 and g >= 2:
                        act.wait_ge(pv_ps, b * G + g - 1)
                    at, width = ST_E[s]
                    act.activation(e_row[g % 2][:, 2 * pr:2 * pr + 2, at:at + width], ps[:, st_bank(m):st_bank(m) + 2, 0:width],
                                   ACT.Exp, scale=SM_SCALE).then_inc(exp_rdy, 1)

                def weighted(g):
                    act.wait_ge(pv_ps, b * G + g + 1)
                    if g >= 1:
                        act.wait_ge(pvT_ps, b * G + g)
                    act.activation(pvs[:], ps[:, 6, :], ACT.Copy).then_inc(pvs_rdy, 1)

                qk_round(0, 0)
                qk_round(0, 1)
                values(0)
                values(1)
                for n in range(STEPS + LAG):
                    m = n - LAG
                    if m >= 0:
                        exps(m)
                    if n in ROUND_AT:
                        qk_round(*ROUND_AT[n])
                    for tb, at in VALUE_AT.items():
                        if n == at + 1:
                            values(tb)
                    if m >= 6 and m % 6 == 0:
                        weighted(m // 6 - 1)
                    if n in (STEPS - 4, STEPS - 2):
                        split_gu(b, (n - STEPS + 4) // 2)
                weighted(G - 1)
                split_d(b, 0)
                act.wait_ge(modsum_rdy, b + 1)
                act.activation(modt[:], modsum[:], ACT.Tanh).then_inc(modt_rdy, 1)
                for f in range(NF):
                    act.wait_ge(gate_ps, b * NF + f + 1)
                    act.activation(th[:], ps[:, 4 + (2 * f) % 3, :], ACT.Tanh, scale=0.5).then_inc(th_rdy, 1)
                    act.wait_ge(prod_rdy, b * NF + f + 1)
                    if f >= 2:
                        act.wait_ge(down_ps, b * (NF - 1) + f - 1)
                    act.activation(act_s[f % 2][0][:], prod[:], ACT.Copy).then_inc(act_hi, 1)
                    if f + 2 < NF:
                        split_gu(b, f + 2)
                    if f + 1 < NF:
                        split_d(b, f + 1)
                    if not last and f in KEYS_AT:
                        kexp_step(b + 1, KEYS_AT.index(f))
                if not last:
                    normed(b + 1)

            with act.Fori(0, NB - 1) as b:
                batch(b, False)
            batch(NB - 1, True)

        @block.vector
        def _(dve):
            own = {"base": 0, "n": 0}

            def mine(op):
                own["n"] += 1
                op.then_inc(dve_own, 1)

            def settled():
                dve.wait_ge(dve_own, own["base"] + own["n"])

            dve.wait_ge(small_ld, 80)
            mine(dve.tensor_scalar(neg_wp[:], w_sb[:], 0.0, -1.0, ALU.max, ALU.mult))
            mine(dve.tensor_scalar(w_minus[:], w_sb[:], 0.0, None, ALU.min))
            settled()
            mine(dve.tensor_tensor(bonus[:], u_sb[:], neg_wp[:], ALU.subtract))
            settled()
            mine(dve.tensor_scalar(bonus[:], bonus[:], BONUS_LOW, None, ALU.max))
            settled()
            dve.tensor_scalar(shift[:], bonus[:], 0.0, SHIFT_LOW, ALU.min, ALU.max).then_inc(prep_rdy, 1)

            def moments(stats, mean, var):
                settled()
                mine(dve.tensor_tensor(half_diff[:], stats[:, :, 1], stats[:, :, 4], ALU.subtract))
                mine(dve.tensor_tensor(mean[:], stats[:, :, 1], stats[:, :, 4], ALU.add))
                mine(dve.tensor_tensor(var[:], stats[:, :, 2], stats[:, :, 5], ALU.add))
                settled()
                mine(dve.scalar_tensor_tensor(half_diff[:], half_diff[:], 0.25, half_diff[:], ALU.mult, ALU.mult))
                mine(dve.tensor_scalar(mean[:], mean[:], 0.5, None, ALU.mult))
                settled()
                mine(dve.scalar_tensor_tensor(var[:], var[:], 1.0 / D, half_diff[:], ALU.mult, ALU.add))
                settled()

            def norm1(n, first):
                dve.wait_ge(x_ld, 16 * (n + 1))
                for tb in range(TB):
                    op = dve.bn_stats(bn6[:, tb, :], x_sb[:, tb, :])
                mine(op)
                moments(bn6, mean, var)
                dve.tensor_scalar(var_eps[:], var[:], LN_EPS, None, ALU.add).then_inc(stats1, 1)

            def norm1_apply(n, first):
                dve.wait_ge(rstd1, n + 1)
                if not first:
                    dve.wait_ge(hnT_ps, n * DB)
                for tb in range(TB):
                    op = dve.tensor_scalar(norm[:, tb, :], x_sb[:, tb, :], mean[:, tb:tb + 1], rstd[:, tb:tb + 1],
                                           ALU.subtract, ALU.mult)
                op.then_inc(xn_rdy, 1)

            def keys(n, cb, first, bank=TPB):
                dve.wait_ge(xnT_ps, n * DB + cb + 1)
                if cb == 0 and not first:
                    dve.wait_ge(pv_ps, n * G)
                if cb >= 2 and not first:
                    dve.wait_ge(yT_rdy, n * DB + cb - 1)
                dve.scalar_tensor_tensor(k_of(cb, first), steps[:], neg_wp[:, cb:cb + 1], ps[:, bank, :],
                                         ALU.mult, ALU.add).then_inc(kt_rdy, 1)

            def scans(n, cb, first=False):
                if cb == 0:
                    dve.memset(p_run[:, 0:1], 0.0)
                    dve.memset(q_run[:, 0:1], 0.0)
                a = decay[:, cb:cb + 1].broadcast_to([P, T])
                dve.wait_ge(kv_rdy, n * DB + cb + 1)
                k, kv_ = k_of(cb, first), kv_of(cb, first)
                dve.tensor_tensor_scan(q_run[:, 1:T + 1], a, k, 0.0, ALU.mult, ALU.add)
                mine(dve.tensor_tensor_scan(p_run[:, 1:T + 1], a, kv_, 0.0, ALU.mult, ALU.add))
                settled()
                dve.scalar_tensor_tensor(k, q_run[:, 0:T], rho[:, cb:cb + 1], k, ALU.mult, ALU.add)
                mine(dve.scalar_tensor_tensor(kv_, p_run[:, 0:T], rho[:, cb:cb + 1], kv_, ALU.mult, ALU.add))

            def recips(n, cb, half=None, first=False):
                settled()
                at = slice(0, T) if half is None else slice(half * T // 2, (half + 1) * T // 2)
                op = dve.reciprocal(k_of(cb, first)[:, at], k_of(cb, first)[:, at])
                if half == 0:
                    mine(op)
                else:
                    op.then_inc(recip_rdy, 1)

            def residual1(n, tb, bank=TPB):
                dve.wait_ge(yT_ps, n * TB + tb + 1)
                dve.scalar_tensor_tensor(x_sb[:, tb, :], ps[:, bank, :], gate_t[:, 0:1], x_sb[:, tb, :],
                                         ALU.mult, ALU.add).then_inc(x1_rdy, 1)
                dve.wait_ge(x1_rdy, n * TB + tb + 1)
                mine(dve.bn_stats(bn6b[:, tb, :], x_sb[:, tb, :]))

            def norm2(n):
                moments(bn6b, meanb, varb)
                dve.tensor_scalar(var_epsb[:], varb[:], LN_EPS, None, ALU.add).then_inc(stats2, 1)
                dve.wait_ge(rstd2, n + 1)
                mine(dve.tensor_tensor(vr[:], varb[:], rstdb[:], ALU.mult))
                settled()
                mine(dve.tensor_tensor(vr[:], vr[:], rstdb[:], ALU.mult))
                settled()
                dve.tensor_scalar(ms_eps[:], vr[:], RMS_EPS, None, ALU.add).then_inc(ms2, 1)
                mine(dve.tensor_scalar(gr[:], rstdb[:], gate_t[:, 1:2], None, ALU.mult))
                settled()
                dve.tensor_scalar(base_mul[:], gr[:], 1.0, None, ALU.add)
                mine(dve.scalar_tensor_tensor(base_add[:], meanb[:], -1.0, gr[:], ALU.mult, ALU.mult))
                dve.wait_ge(rms2, n + 1)
                mine(dve.tensor_tensor(hn_scale[:], rstdb[:], rms[:], ALU.mult))
                settled()
                dve.wait_ge(xnT_ps, (n + 1) * DB)
                for tb in range(TB):
                    op = dve.tensor_scalar(norm[:, tb, :], x_sb[:, tb, :], meanb[:, tb:tb + 1], hn_scale[:, tb:tb + 1],
                                           ALU.subtract, ALU.mult)
                op.then_inc(hn_rdy, 1)

            norm1(0, True)
            norm1_apply(0, True)
            dve.wait_ge(decay_rdy, 1)
            dve.tensor_scalar(half_gate[:], gate_t[:, 1:2], 0.5, None, ALU.mult)
            dve.wait_ge(const_rdy, 5)
            for cb in range(DB):
                keys(0, cb, True, 4 + cb)
            for cb in range(DB):
                scans(0, cb, True)
                recips(0, cb, None, True)
                if cb == 0:
                    mine(dve.memset(woa[:], 0.0))
                    dve.wait_ge(woa_ps, 1)
                    settled()
                    for j in range(4):
                        op = dve.tensor_copy(woa[quad(j), :, R * j:R * j + R], ps[quad(j), 0, 0:DB * R].rearrange("p (t r) -> p t r", r=R))
                    op.then_inc(woa_sb, 1)
            dve.wait_ge(ga_hi, DB)
            for db in range(DB):
                dve.scalar_tensor_tensor(ga_s[1][:, db, 0:H * R], ps[:, 2 + db // 2, 256 * (db % 2):256 * (db % 2) + 256],
                                         ln1_sb[:, db:db + 1], f32(ga_s[0][:, db, 0:H * R]), ALU.mult, ALU.subtract)
                dve.scalar_tensor_tensor(ga_s[1][:, db, H * R:GA], a_sb[:, db, :], ln2_sb[:, db:db + 1],
                                         f32(ga_s[0][:, db, H * R:GA]), ALU.mult, ALU.subtract).then_inc(ga_lo, 1)
            for tb in range(TB):
                residual1(0, tb, 4 + tb)
            norm2(0)
            own_prologue = own["n"]

            def normed(n):
                for db in range(DB):
                    dve.wait_ge(hn_hi, n * DB + db + 1)
                    dve.tensor_tensor(hn_s[1][:, db, :], ps[:, HB[db], :], f32(hn_s[0][:, db, :]), ALU.subtract).then_inc(hn_lo, 1)
                for i, db in enumerate(H_ORDER):
                    dve.wait_ge(h_hi, n * DB + i + 1)
                    dve.scalar_tensor_tensor(h_s[1][:, db, :], ps[:, HB[db], :], ln2_sb[:, db:db + 1], f32(h_s[0][:, db, :]),
                                             ALU.mult, ALU.subtract).then_inc(h_lo, 1)

            def finish(b):
                for tb in range(TB):
                    dve.wait_ge(mlp_ps, b * TB + tb + 1)
                    dve.scalar_tensor_tensor(base[:, tb, :], ps[:, tb, :], half_gate[:], base[:, tb, :],
                                             ALU.mult, ALU.add).then_inc(fin_rdy, 1)

            normed(0)

            def make_base(b):
                dve.wait_ge(base_free, 64 * (b + 1))
                for tb in range(TB):
                    op = dve.tensor_scalar(base[:, tb, :], x_sb[:, tb, :], base_mul[:, tb:tb + 1], base_add[:, tb:tb + 1],
                                           ALU.mult, ALU.add)
                op.then_inc(base_rdy, 1)

            def batch(b, last):
                own["base"], own["n"] = own_prologue + b * DVE_OWN_PER_BATCH, 0

                def qk_low(g, i, heads=range(4)):
                    st, at = ((q_st, 32), (k_st, 64))[i]
                    for j in heads:
                        dve.wait_ge(qk_hi, b * 8 * G + 8 * g + 4 * i + j + 1)
                        op = dve.tensor_tensor(st[g % 3][at:at + 32, j, :], ps[quad(j), 4 + i, :], f32(st[g % 3][0:32, j, :]), ALU.subtract)
                    if 3 in heads:
                        op.then_inc(qk_lo, 1)

                def maxima(n):
                    g, s, pr = n // 6, n % 6 // 2, n % 2
                    if n % 6 == 0 and g >= 1:
                        dve.wait_ge(nmc_rdy, b * G + g)
                    for i in range(2):
                        j = 2 * pr + i
                        dve.wait_ge(s_ps, 2 * (b * STEPS + n) + i + 1)
                        for at, qb in S_STEPS[s]:
                            op = dve.reduce_max(mx[:, qb, j:j + 1], ps[:, i, at:at + (qb + 1) * P], AX.X)
                        op.then_inc(smax_rdy, 1)
                        for lg, li, j0 in LOW_AT.get(n, ()):
                            qk_low(lg, li, (j0 + i,))

                def minus_max(g):
                    dve.wait_ge(smax_rdy, 2 * (b * STEPS + 6 * g + 6))
                    mine(dve.tensor_scalar(nmc[:, :, 0:4].bitcast(F32R), mx[:], -1.0, None, ALU.mult))
                    settled()
                    dve.scalar_tensor_tensor(nmc[:, :, 4:8], mx[:], -1.0, nmc[:, :, 0:4], ALU.mult, ALU.subtract).then_inc(nmc_rdy, 1)

                def minus_max_rows(g):
                    dve.wait_ge(nm_ps, b * G + g + 1)
                    if g >= 1:
                        dve.wait_ge(nm_ld[g - 1], 32 * (b + 1))
                    dve.tensor_copy(nmrow[:], ps[0:8, TPB, :]).then_inc(nmrow_rdy, 1)

                def weighted(g):
                    dve.wait_ge(pvT_ps, b * G + g + 1)
                    pvT = ps[:, TPB, :].rearrange("p (q j c) -> p q j c", q=TB, j=4)
                    mine(dve.reciprocal(rl[:], pvT[:, :, :, R]))
                    settled()
                    for qb in range(TB):
                        op = dve.tensor_tensor(pvn[:, qb, :, :], pvT[:, qb, :, 0:R], rl[:, qb, :].unsqueeze(2).broadcast_to([P, 4, R]), ALU.mult)
                    op.then_inc(pvT_used, 1)
                    dve.wait_ge(pvT_used, b * G + g + 1)
                    mine(dve.reduce_sum(modp[:, g, :, :], pvn[:].rearrange("p q j r -> p q r j"), AX.X))

                qk_low(0, 0)
                qk_low(0, 1)
                for n in range(STEPS + LAG):
                    if n < STEPS:
                        maxima(n)
                    if n % 6 == 5 and n < STEPS:
                        minus_max(n // 6)
                    if n % 6 == 0 and 6 <= n <= STEPS:
                        minus_max_rows(n // 6 - 1)
                    if n == BASE_AT:
                        make_base(b)
                    if n >= NORM_LAG and (n - NORM_LAG) % 6 == 0:
                        weighted((n - NORM_LAG) // 6)
                weighted(G - 1)
                settled()
                dve.reduce_sum(modsum[:], modp[:].rearrange("p g q r -> p q r g"), AX.X).then_inc(modsum_rdy, 1)
                dve.wait_ge(modt_rdy, b + 1)
                mine(dve.scalar_tensor_tensor(t_mod[:], modt[:], MOD_SCALE, h_a[:], ALU.mult, ALU.mult))
                settled()
                dve.tensor_copy(tcols[:, :, 0:R].bitcast(F32R), t_mod[:])
                mine(dve.tensor_copy(tcols[:, :, 4 * R:5 * R].bitcast(F32R), t_mod[:]))
                settled()
                dve.tensor_tensor(tcols[:, :, 2 * R:3 * R], t_mod[:], tcols[:, :, 0:R], ALU.subtract).then_inc(t_rdy, 1)
                dve.wait_ge(tT_ps, b + 1)
                dve.tensor_copy(t_s[:], ps[0:5 * R, TPB, :]).then_inc(tT_rdy, 1)

                for f in range(NF):
                    dve.wait_ge(th_rdy, b * NF + f + 1)
                    if f >= 1:
                        dve.wait_ge(prod_rdy, b * NF + f)
                    dve.scalar_tensor_tensor(gsil[:], th[:], 1.0, ps[:, 4 + (2 * f) % 3, :], ALU.add, ALU.mult).then_inc(gsil_rdy, 1)
                    dve.wait_ge(up_ps, b * NF + f + 1)
                    dve.wait_ge(gsil_rdy, b * NF + f + 1)
                    if f >= 1:
                        dve.wait_ge(act_lo, b * NF + f)
                    dve.tensor_tensor(prod[:], gsil[:], ps[:, 4 + (2 * f + 1) % 3, :], ALU.mult).then_inc(prod_rdy, 1)
                    dve.wait_ge(act_hi, b * NF + f + 1)
                    dve.tensor_tensor(act_s[f % 2][1][:], prod[:], f32(act_s[f % 2][0][:]), ALU.subtract).then_inc(act_lo, 1)
                    if not last:
                        n = b + 1
                        if f == 0:
                            norm1(n, False)
                        if f == 1:
                            norm1_apply(n, False)
                        for cb in range(DB):
                            if f == RECIP_AT[cb][1] and RECIP_AT[cb][0] < f:
                                recips(n, cb, 1)
                        for cb in range(DB):
                            if f == SCANS_AT[cb]:
                                if f == KEYS_AT[(cb + 1) % DB]:
                                    keys(n, cb + 1, False)
                                scans(n, cb)
                        for cb in range(DB):
                            if f == RECIP_AT[cb][0]:
                                recips(n, cb, 0 if RECIP_AT[cb][1] > f else None)
                        if f in KEYS_AT and f not in SCANS_AT:
                            keys(n, KEYS_AT.index(f), False)
                        if Y_AT <= f < Y_AT + TB:
                            residual1(n, f - Y_AT)
                        if f == NORM2_AT:
                            norm2(n)
                if not last:
                    normed(b + 1)
                finish(b)
                assert last or own["n"] == DVE_OWN_PER_BATCH, own["n"]

            with dve.Fori(0, NB - 1) as b:
                batch(b, False)
            batch(NB - 1, True)

        @block.tensor
        def _(pe):
            def split_matmul(dst, w_hi, w_lo, m_hi, m_lo, start, stop):
                pe.matmul(dst, w_hi, m_hi, start=start, stop=False)
                pe.matmul(dst, w_hi, m_lo, start=False, stop=False)
                return pe.matmul(dst, w_lo, m_hi, start=False, stop=stop)

            def keys_T(n, cb, bank=TPB, shared=True):
                pe.wait_ge(xn_rdy, n + 1)
                if cb >= 1 and shared:
                    pe.wait_ge(kt_rdy, n * DB + cb)
                for tb in range(TB):
                    op = pe.transpose(ps[:, bank, blk(tb)], norm[:, tb, blk(cb)], ident[:])
                op.then_inc(xnT_ps, 1)

            def rows_y(n, tb, bank=TPB, shared=True):
                pe.wait_ge(yT_rdy, (n + 1) * DB)
                if tb >= 1 and shared:
                    pe.wait_ge(x1_rdy, n * TB + tb)
                for cb in range(DB):
                    op = pe.transpose(ps[:, bank, blk(cb)], yT[:, cb, blk(tb)], ident[:])
                op.then_inc(yT_ps, 1)

            def normed_T(n, db):
                pe.wait_ge(hn_rdy, n + 1)
                for tb in range(TB):
                    op = pe.transpose(ps[:, HB[db], blk(tb)], norm[:, tb, blk(db)], ident[:])
                op.then_inc(hnT_ps, 1)

            pe.wait_ge(const_rdy, 6)
            for cb in range(DB):
                keys_T(0, cb, 4 + cb, False)
            pe.wait_ge(woa_ld, 48)
            for jt in range(DB):
                for ot in range(DB):
                    op = pe.matmul(ps[:, 0, R * jt:R * jt + R], raw_wo[:, ot, blk(jt)], a_sb[:, ot, :],
                                   start=ot == 0, stop=ot == DB - 1)
            op.then_inc(woa_ps, 1)
            pe.wait_ge(woa_sb, 1)
            for db in range(DB):
                for jt in range(DB):
                    at = 256 * (db % 2) + 4 * R * jt
                    op = pe.matmul(ps[:, 2 + db // 2, at:at + 4 * R], raw_wv[:, jt, blk(db)], woa[:, jt, :], start=True, stop=True)
            op.then_inc(ga_ps, 1)
            for tb in range(TB):
                rows_y(0, tb, 4 + tb, False)
            for db in range(DB):
                normed_T(0, db)
            pe.wait_ge(wsplit_lo, 2 * DB)
            pe.wait_ge(ones_rdy, 3)
            pe.wait_ge(const_rdy, 8)

            def batch(b, last):
                def project(g, i, dbs=range(DB)):
                    w = (wq_s, wk_s)[i]
                    if g == 0:
                        pe.wait_ge(h_lo, b * DB + i + 1)
                    elif 0 in dbs:
                        pe.wait_ge(qk_lo, b * 2 * G + 2 * (g - 1) + i + 1)
                    for db in dbs:
                        op = split_matmul(ps[:, 4 + i, :], w[0][:, db, blk(g)], w[1][:, db, blk(g)], hn_s[0][:, db, :], hn_s[1][:, db, :],
                                          db == 0, db == DB - 1)
                    if DB - 1 in dbs:
                        op.then_inc(qk_ps, 1)

                def values(tb):
                    if tb < 2:
                        pe.wait_ge(h_lo, b * DB + 2 + tb + 1)
                    else:
                        pe.wait_ge(va_sb, b * TB + 2)
                    for db in range(DB):
                        op = split_matmul(ps[:, VALUE_BANK[tb], 0:GA], hn_s[0][:, db, blk(tb)], hn_s[1][:, db, blk(tb)],
                                          ga_s[0][:, db, :], ga_s[1][:, db, :], db == 0, db == DB - 1)
                    op.then_inc(va_ps, 1)

                def scores(n):
                    g, s, pr = n // 6, n % 6 // 2, n % 2
                    if n % 6 == 0:
                        pe.wait_ge(rep_ld[g], 32 * (b + 1))
                        pe.wait_ge(qk_lo, b * 2 * G + 2 * g + 2)
                    for i in range(2):
                        j = 2 * pr + i
                        if n >= 1:
                            pe.wait_ge(smax_rdy, 2 * (b * STEPS + n) + i - 1)
                        for at, qb in S_STEPS[s]:
                            w = (qb + 1) * P
                            pe.matmul(ps[:, i, at:at + w], q_st[g % 3][0:96, j, blk(qb)], k_st[g % 3][0:96, j, 0:w], start=True, stop=False)
                            op = pe.matmul(ps[:, i, at + w - P:at + w], identb[:], mask_qk[:], start=False, stop=True)
                        op.then_inc(s_ps, 1)

                def scores_T(m):
                    g, s, pr = m // 6, m % 6 // 2, m % 2
                    if m % 6 == 0:
                        pe.wait_ge(nm_ld[g], 32 * (b + 1))
                    if m == TWO_PAIRS:
                        pe.wait_ge(smax_rdy, 2 * (b + 1) * STEPS)
                    elif m >= 1:
                        pe.wait_ge(exp_rdy, b * STEPS + (m if m < TWO_PAIRS else m - 1))
                    for at, kb in ST_STEPS[s]:
                        w = T - kb * P
                        for i in range(2):
                            pe.matmul(ps[:, st_bank(m) + i, at:at + w], k_st[g % 3][0:98, 2 * pr + i, blk(kb)],
                                      q_st[g % 3][0:98, 2 * pr + i, kb * P:T], start=True, stop=False)
                        for i in range(2):
                            op = pe.matmul(ps[:, st_bank(m) + i, at:at + P], identb[:], mask_kq[:], start=False, stop=True)
                    op.then_inc(st_ps, 1)

                def maxima_T(g):
                    pe.wait_ge(nmc_rdy, b * G + g + 1)
                    if g == 0:
                        pe.wait_ge(va_sb, b * TB + 3)
                    else:
                        pe.wait_ge(nmrow_rdy, b * G + g)
                    if g >= 2:
                        pe.wait_ge(pvT_used, b * G + g - 1)
                    for qb in range(TB):
                        op = pe.transpose(ps[0:8, TPB, blk(qb)], nmc[:, qb, :], ident[:])
                    op.then_inc(nm_ps, 1)

                def weigh(g):
                    pe.wait_ge(exp_rdy, b * STEPS + 6 * g + 6)
                    if g == 0:
                        pe.wait_ge(va_sb, (b + 1) * TB)
                    else:
                        pe.wait_ge(pvs_rdy, b * G + g)
                    for kb in range(TB):
                        w = T - kb * P
                        for j in range(4):
                            op = pe.matmul(ps[quad(j), 6, kb * P:T], v_aug[:, kb, 4 * g + j, :], e_row[g % 2][:, j, E_AT[kb]:E_AT[kb] + w],
                                           start=kb == 0, stop=kb == TB - 1)
                    op.then_inc(pv_ps, 1)

                def weighed_T(g):
                    pe.wait_ge(pvs_rdy, b * G + g + 1)
                    pe.wait_ge(nmrow_rdy, b * G + min(g + 2, G))
                    if g == G - 1:
                        pe.wait_ge(pvT_used, b * G + g)
                    for qb in range(TB):
                        op = pe.transpose(ps[:, TPB, blk(qb)], pvs[:, blk(qb)], ident[:])
                    op.then_inc(pvT_ps, 1)

                def gate(f, dbs=range(DB)):
                    if 0 in dbs:
                        if f == 0:
                            pe.wait_ge(qk_lo, (b + 1) * 2 * G)
                        elif f >= 2:
                            pe.wait_ge(prod_rdy, b * NF + f - 1)
                        pe.wait_ge(gu_lo, b * NF + f + 1)
                    for db in dbs:
                        split_matmul(ps[:, 4 + (2 * f) % 3, :], gu_s[f % 2][0][:, blk(db)], gu_s[f % 2][1][:, blk(db)],
                                     h_s[0][:, db, :], h_s[1][:, db, :], db == 0, False)

                def gate_mod(f):
                    if f == 0:
                        pe.wait_ge(base_free, 64)
                        pe.wait_ge(tT_rdy, b + 1)
                    pe.matmul(ps[:, 4 + (2 * f) % 3, :], b_s[:, blk(f)], t_s[:], start=False, stop=True).then_inc(gate_ps, 1)

                def up(f, dbs=range(DB)):
                    if f >= 1:
                        pe.wait_ge(gsil_rdy, b * NF + f)
                    for db in dbs:
                        op = split_matmul(ps[:, 4 + (2 * f + 1) % 3, :], gu_s[f % 2][0][:, D + db * P:D + (db + 1) * P],
                                          gu_s[f % 2][1][:, D + db * P:D + (db + 1) * P],
                                          h_s[0][:, db, :], h_s[1][:, db, :], db == 0, db == DB - 1)
                    if DB - 1 in dbs:
                        op.then_inc(up_ps, 1)

                def down(f):
                    pe.wait_ge(act_lo, b * NF + f + 1)
                    pe.wait_ge(wd_lo, b * NF + f + 1)
                    for tb in range(TB):
                        op = split_matmul(ps[:, tb, :], act_s[f % 2][0][:, blk(tb)], act_s[f % 2][1][:, blk(tb)],
                                          wd_s[f % 2][0][:], wd_s[f % 2][1][:], f == 0, f == NF - 1)
                        if f == NF - 1:
                            op.then_inc(mlp_ps, 1)
                    if f < NF - 1:
                        op.then_inc(down_ps, 1)

                pe.wait_ge(hn_lo, (b + 1) * DB)
                project(0, 0)
                project(0, 1)
                pe.wait_ge(ga_lo, DB)
                values(0)
                values(1)
                for n in range(min(PROJ_AT.values()), STEPS + LAG):
                    if 0 <= n < STEPS:
                        scores(n)
                    if n % 6 == 0 and 6 <= n <= STEPS:
                        maxima_T(n // 6 - 1)
                    for g, at in PROJ_AT.items():
                        if at <= n < at + 4:
                            project(g, (n - at) // 2, ((0, 1), (2, 3))[(n - at) % 2])
                    for tb, at in VALUE_AT.items():
                        if n == at:
                            values(tb)
                    m = n - LAG
                    if m == STEPS - 6:
                        gate(0)
                    if m >= 0:
                        scores_T(m)
                    if m >= 6 and m % 6 == 0:
                        weigh(m // 6 - 1)
                    if m >= 7 and m % 6 == 1:
                        weighed_T(m // 6 - 1)
                    if m in (STEPS - 4, STEPS - 2):
                        up(0, ((m - STEPS + 4) // 2,))
                up(0, (2,))
                weigh(G - 1)
                weighed_T(G - 1)
                gate(1, (0, 1, 2))
                pe.wait_ge(t_rdy, b + 1)
                for tb in range(TB):
                    op = pe.transpose(ps[0:5 * R, TPB, blk(tb)], tcols[:, tb, :], ident[:])
                op.then_inc(tT_ps, 1)
                up(0, (3,))
                gate_mod(0)
                gate(1, (3,))
                gate_mod(1)

                for f in range(NF):
                    if f >= 2:
                        gate(f)
                        gate_mod(f)
                    if f >= 1:
                        up(f)
                    if not last and f in KEYS_AT:
                        keys_T(b + 1, KEYS_AT.index(f))
                    if not last and Y_AT <= f < Y_AT + TB:
                        rows_y(b + 1, f - Y_AT)
                    if not last and f == NF - 1:
                        pe.wait_ge(prod_rdy, b * NF + f)
                        for db in (0, 1):
                            normed_T(b + 1, db)
                    if f >= 1:
                        down(f - 1)
                if not last:
                    pe.wait_ge(prod_rdy, (b + 1) * NF)
                    for db in (2, 3):
                        normed_T(b + 1, db)
                down(NF - 1)

            with pe.Fori(0, NB - 1) as b:
                batch(b, False)
            batch(NB - 1, True)


def kernel(x, ctx_2048, g_xattn, g_ffn, L0_xattn_w, L0_xattn_u, L0_ffn_ln1_w, L0_ffn_ln2_w, L0_ffn_Wq, L0_ffn_Wk,
           L0_ffn_Wv, L0_ffn_Wo, L0_ffn_A, L0_ffn_B, L0_ffn_W_in_base, L0_ffn_W_up_base, L0_ffn_W_down):
    from concourse import bacc
    from concourse.bass_utils import run_bass_kernel_spmd

    a = np.asarray
    col = lambda v: np.ascontiguousarray(a(v).reshape(DB, P).T)
    tiles = lambda m: a(m).reshape(NF, P, DB, P).transpose(0, 3, 2, 1)
    w_gu = np.ascontiguousarray(np.stack([tiles(L0_ffn_W_in_base), tiles(L0_ffn_W_up_base)], axis=2).reshape(NF, P, 2 * D))
    arrays = {
        "x": a(x),
        "ctxT": np.ascontiguousarray(a(ctx_2048).transpose(0, 2, 1)),
        "w4": col(L0_xattn_w), "u4": col(L0_xattn_u),
        "gates": np.ascontiguousarray(np.broadcast_to(np.concatenate([a(g_xattn), a(g_ffn)])[None, :], (P, 2))),
        "ln1": col(L0_ffn_ln1_w), "ln2": col(L0_ffn_ln2_w),
        "wqT": np.ascontiguousarray(a(L0_ffn_Wq).T), "wkT": np.ascontiguousarray(a(L0_ffn_Wk).T),
        "wv": a(L0_ffn_Wv), "wo": a(L0_ffn_Wo), "a4": a(L0_ffn_A), "b_mod": a(L0_ffn_B),
        "w_gu": w_gu, "w_down": np.ascontiguousarray(a(L0_ffn_W_down).T),
    }
    arrays = {f"{k}_dram": np.ascontiguousarray(v) for k, v in arrays.items()}
    nc = bacc.Bacc("TRN2", target_bir_lowering=False, num_devices=1, dynamic_dma_scratch_size=DGE_SCRATCH)
    args = [nc.dram_tensor(k, v.shape, F32, kind="ExternalInput").ap() for k, v in arrays.items()]
    args.append(nc.dram_tensor("out_dram", (NB, T, D), F32, kind="ExternalOutput").ap())
    flamingo_layer(nc, *args)
    return run_bass_kernel_spmd(nc, [arrays], core_ids=[0]).results[0]["out_dram"]
```

```python
from contextlib import ExitStack

import numpy as np

import concourse.bass as bass
import concourse.mybir as mybir

F32, F32R, BF16 = mybir.dt.float32, mybir.dt.float32r, mybir.dt.bfloat16
ALU, ACT, AX = mybir.AluOpType, mybir.ActivationFunctionType, mybir.AxisListType

NB, T, D = 4, 512, 512
FF, R, H = 2048, 16, 16
HD = D // H
P = 128
TB, DB = T // P, D // P
NF = FF // P
G = H // 4
VW = 32
GA = H * R + R
LN_EPS, RMS_EPS = 1e-5, 1e-6
MASKED = -1e30
SM_SCALE = float(1.0 / np.sqrt(np.float32(HD)))
MOD_SCALE = 0.1
BONUS_LOW, SHIFT_LOW = -70.0, -40.0
DGE_SCRATCH = 1024
DVE_OWN_PER_BATCH = 42

E_AT = [0, 640, 1024, 512]
S_STEPS = [[(0, 3)], [(P, 2), (0, 0)], [(0, 1)]]
ST_STEPS = [[(0, 0)], [(P, 1), (0, 3)], [(0, 2)]]
ST_E = [(0, 512), (512, 512), (1024, 256)]

STEPS = 6 * G
LAG = 8
PROJ_AT = {1: -2, 2: 3, 3: 10}
STAGED = 2
ROUND_AT = (0, 2)
LOW_HALF = (0, 1, 2, 3, 4, 5, 6, 7)
STAGE_AT = {2: (5, 7), 3: (12, 14)}
LOW_AT = {2: (6, 8), 3: (12, 14)}
COPY_AT = {2: (5, 8), 3: (13, 15)}
NORM_LAG = LAG + 9
SPLIT_AT = (20, 22)
BASE_AT = 4
TWO_PAIRS = 17
st_bank = lambda m: 0 if m >= TWO_PAIRS and m % 2 else 2
s_bank = lambda n: 2 if n < LAG and n % 2 else 0
VALUE_BANK = [6, 7, 7, 6]
VALUE_AT = {2: 2, 3: 3}
HB = [6, 7, 4, 5]
H_ORDER = [2, 3, 0, 1]
KEYS_AT, SCANS_AT, RECIP_AT = [2, 3, 5, 6], [3, 4, 6, 7], [(3, 4), (5, 5), (6, 7), (8, 8)]
Y_AT, NORM2_AT = 9, 13


def flamingo_layer(nc, x, ctxT, w4, u4, gates, ln1, ln2, wqT, wkT, wv, wo, a4, b_mod, w_gu, w_down, out):
    es = ExitStack()
    with es:
        top = [nc.sbuf_base + (-nc.sbuf_base) % 64]

        def place(name, shape, dt, at=None):
            size = int(np.prod(shape[1:])) * (2 if dt == BF16 else 4)
            size += -size % 32
            off = top[0] if at is None else at[0]
            if at is None:
                top[0] += size
            else:
                at[0] += size
                assert at[0] <= at[1], name
            return nc.alloc_sbuf_tensor_at(name, shape, dt, offset=off)

        def region(size):
            at = top[0]
            top[0] += size
            return [at, at + size]

        def sem(name):
            return es.enter_context(nc.semaphore(name))

        ident = place("ident", [P, P], F32)
        identb = place("identb", [P, P], BF16)
        mask_qk = place("mask_qk", [P, P], BF16)
        mask_kq = place("mask_kq", [P, P], BF16)
        steps = place("steps", [P, T], F32)
        w_sb = place("w_sb", [P, DB], F32)
        u_sb = place("u_sb", [P, DB], F32)
        gates_sb = place("gates_sb", [P, 2], F32)
        ln1_sb = place("ln1_sb", [P, DB], F32)
        ln2_sb = place("ln2_sb", [P, DB], F32)
        a_sb = place("a_sb", [P, DB, R], F32)
        neg_wp = place("neg_wp", [P, DB], F32)
        w_minus = place("w_minus", [P, DB], F32)
        decay = place("decay", [P, DB], F32)
        bonus = place("bonus", [P, DB], F32)
        shift = place("shift", [P, DB], F32)
        rho = place("rho", [P, DB], F32)
        gate_t = place("gate_t", [P, 2], F32)
        half_gate = place("half_gate", [P, 1], F32)
        minus_half = place("minus_half", [P, TB], F32)
        wq_s = [place(f"wq_{n}", [P, DB, D], F32R) for n in ("hi", "lo")]
        wk_s = [place(f"wk_{n}", [P, DB, D], F32R) for n in ("hi", "lo")]
        ga_s = [place(f"ga_{n}", [P, DB, GA], F32R) for n in ("hi", "lo")]
        b_s = place("b_s", [5 * R, FF], F32R)
        v_aug = place("v_aug", [P, TB, H, VW], F32)
        k_st = [place(f"k_st{i}", [P, 4, T], F32R) for i in range(3)]
        base_at = region(8192)
        raw_b = place("raw_b", [5 * R, FF], F32, list(base_at))
        base = place("base", [P, TB, D], F32, base_at)
        h_at = region(16384)
        first_at = list(h_at)
        h_s = [place(f"h_{n}", [P, DB, T], F32R, h_at) for n in ("hi", "lo")]
        raw_gu = [place(f"raw_gu{i}", [P, 2 * D], F32) for i in range(2)]
        raw_d = [place(f"raw_d{i}", [P, D], F32) for i in range(2)]
        bn6 = place("bn6", [P, TB, 6], F32)
        mean = place("mean", [P, TB], F32)
        var = place("var", [P, TB], F32)
        half_diff = place("half_diff", [P, TB], F32)
        var_eps = place("var_eps", [P, TB], F32)
        rstd = place("rstd", [P, TB], F32)
        bn6b = place("bn6b", [P, TB, 6], F32)
        meanb = place("meanb", [P, TB], F32)
        varb = place("varb", [P, TB], F32)
        var_epsb = place("var_epsb", [P, TB], F32)
        rstdb = place("rstdb", [P, TB], F32)
        var_both = place("var_both", [P, TB], F32)
        hn_scale = place("hn_scale", [P, TB], F32)
        gr = place("gr", [P, TB], F32)
        base_mul = place("base_mul", [P, TB], F32)
        base_add = place("base_add", [P, TB], F32)
        mx = place("mx", [P, TB, 4], F32)
        nmc = place("nmc", [P, TB, 8], F32)
        nmrow = place("nmrow", [8, T], F32R)
        qk_hi4 = place("qk_hi4", [P, T], F32R)
        qk_lo4 = [place(f"{n}_lo4", [P, T], F32R) for n in "qk"]
        pvs = place("pvs", [P, T], F32)
        rl = place("rl", [P, TB, 4], F32)
        pvn = [place(f"pvn{i}", [P, TB, 5, R], F32) for i in range(2)]
        modsum = place("modsum", [P, TB, R], F32)
        modt = place("modt", [P, TB, R], F32)
        h_a = place("h_a", [P, TB, R], F32)
        t_mod = place("t_mod", [P, TB, R], F32)
        tcols = place("tcols", [P, TB, 5 * R], F32)
        t_s = place("t_s", [5 * R, T], F32R)

        wide = region(24576 + 2 * 8192)
        e_at = [wide[0] + 16384, wide[1]]
        r2 = [wide[0], wide[0] + 24576]
        norm_at = [r2[1], r2[1] + 8192]
        x_at = [norm_at[1], norm_at[1] + 8192]
        norm = place("norm", [P, TB, D], F32, norm_at)
        x_sb = place("x_sb", [P, TB, D], F32, x_at)
        r2a, r2s = list(r2), list(r2)
        hn_s = [place(f"hn_{n}", [P, DB, T], F32R, r2a) for n in ("hi", "lo")]
        raw_wq = place("raw_wq", [P, DB, D], F32, r2s)
        raw_wk = place("raw_wk", [P, DB, D], F32, r2s)
        raw_wv = place("raw_wv", [P, DB, D], F32, r2s)
        gu_s = [[place(f"gu{i}_{n}", [P, 2 * D], F32R, r2) for n in ("hi", "lo")] for i in range(2)]
        wd_s = [[place(f"wd{i}_{n}", [P, D], F32R, r2) for n in ("hi", "lo")] for i in range(2)]
        r1 = region(45056)
        r1a = list(r1)
        q_st = [place(f"q_st{i}", [P, 4, T], F32R, r1a) for i in range(3)]
        e_row = [place("e_row0", [P, 4, 1280], F32, r1a), place("e_row1", [P, 4, 1280], F32, e_at)]
        vT = place("vT", [P, DB, T], F32, r1)
        kexp = [place(f"kexp{i}", [P, T], F32, r1 if i < 2 else first_at) for i in range(4)]
        kv = [place(f"kv{i}", [P, T], F32, r1 if i < 2 else first_at) for i in range(4)]
        p_run = place("p_run", [P, T + 1], F32, r1)
        q_run = place("q_run", [P, T + 1], F32, r1)
        yT = place("yT", [P, DB, T], F32, r1)
        r1s = list(r1)
        raw_wo = place("raw_wo", [P, DB, D], F32, r1s)
        woa = place("woa", [P, DB, 4 * R], F32, r1s)
        th = place("th", [P, T], F32, r1)
        gsil = place("gsil", [P, T], F32, r1)
        prod = place("prod", [P, T], F32, r1)
        act_s = [[place(f"act{i}_{n}", [P, T], F32R, r1) for n in ("hi", "lo")] for i in range(2)]
        assert top[0] <= nc.sbuf_usable_end, (top[0], nc.sbuf_usable_end)

        ps = es.enter_context(nc.psum_tensor("ps", [P, 8, 512], F32))
        TPB = 7

        w_ld, woa_ld, b_ld = sem("w_ld"), sem("woa_ld"), sem("b_ld")
        small_ld, v_ld = sem("small_ld"), sem("v_ld")
        x_ld = [sem(f"x_ld{i}") for i in range(TB)]
        gu_ld = [sem(f"gu_ld{i}") for i in range(2)]
        d_ld = [sem(f"d_ld{i}") for i in range(2)]
        rep_ld = [sem(f"rep_ld{i}") for i in range(G)]
        nm_ld = [sem(f"nm_ld{i}") for i in range(G)]
        base_free = sem("base_free")
        const_rdy, prep_rdy, pool_own = sem("const_rdy"), sem("prep_rdy"), sem("pool_own")
        decay_rdy, ones_rdy = sem("decay_rdy"), sem("ones_rdy")
        woa_ps, ga_ps, woa_sb, wscaled, wsplit_hi, wsplit_lo, ga_hi, ga_lo = (sem(n) for n in (
            "woa_ps", "ga_ps", "woa_sb", "wscaled", "wsplit_hi", "wsplit_lo", "ga_hi", "ga_lo"))
        stats1, rstd1, xn_rdy, xnT_ps, kt_rdy, kexp_rdy, kv_rdy, recip_rdy, yT_rdy, yT_ps, x1_rdy = (sem(n) for n in (
            "stats1", "rstd1", "xn_rdy", "xnT_ps", "kt_rdy", "kexp_rdy", "kv_rdy", "recip_rdy", "yT_rdy", "yT_ps", "x1_rdy"))
        stats2, scale2, rstd2, base_scale, hn_rdy, base_rdy, hnT_ps, hn_hi, hn_lo, h_hi, h_lo = (sem(n) for n in (
            "stats2", "scale2", "rstd2", "base_scale", "hn_rdy", "base_rdy", "hnT_ps", "hn_hi", "hn_lo", "h_hi", "h_lo"))
        qk_ps, qk_stage, qk_hi, qk_lo, va_ps, va_sb, s_ps, smax_rdy, nmc_rdy, nm_ps, nmrow_rdy = (sem(n) for n in (
            "qk_ps", "qk_stage", "qk_hi", "qk_lo", "va_ps", "va_sb", "s_ps", "smax_rdy", "nmc_rdy", "nm_ps", "nmrow_rdy"))
        st_ps, exp_rdy, pv_ps, pvs_rdy, pvT_ps, pvT_used, modsum_rdy, modt_rdy, t_rdy, tT_ps, tT_rdy = (sem(n) for n in (
            "st_ps", "exp_rdy", "pv_ps", "pvs_rdy", "pvT_ps", "pvT_used", "modsum_rdy", "modt_rdy", "t_rdy", "tT_ps", "tT_rdy"))
        gu_hi, gu_lo, wd_hi, wd_lo, gate_ps, up_ps, down_ps, th_rdy, gsil_rdy, prod_rdy, act_hi, act_lo, mlp_ps, fin_rdy = (sem(n) for n in (
            "gu_hi", "gu_lo", "wd_hi", "wd_lo", "gate_ps", "up_ps", "down_ps", "th_rdy", "gsil_rdy", "prod_rdy", "act_hi", "act_lo", "mlp_ps", "fin_rdy"))
        dve_own = sem("dve_own")

        f32 = lambda ap: ap.bitcast(F32)
        blk = lambda i: slice(i * P, (i + 1) * P)
        quad = lambda j: slice(32 * j, 32 * j + 32)

        k_of = lambda cb, first: kexp[cb if first else cb % 2][:]
        kv_of = lambda cb, first: kv[cb if first else cb % 2][:]

        block = es.enter_context(nc.Block())

        @block.sync
        def _(sp):
            def load_x(n):
                for tb in range(TB):
                    sp.dma_start(x_sb[:, tb, :], x[bass.ds(n, 1), blk(tb), :].rearrange("o p d -> (o p) d")).then_inc(x_ld[tb], 16)

            def load_v(n):
                sp.dma_start(vT[:], ctxT[bass.ds(n, 1), :, :].rearrange("o (cb p) t -> p (o cb) t", p=P)).then_inc(v_ld, 16)

            def load_gu(f):
                sp.dma_start(raw_gu[f % 2][:], w_gu[f]).then_inc(gu_ld[f % 2], 16)

            def load_d(f):
                sp.dma_start(raw_d[f % 2][:], w_down[blk(f), :]).then_inc(d_ld[f % 2], 16)

            load_x(0)
            for dst, src in ((w_sb, w4), (u_sb, u4), (gates_sb, gates), (ln1_sb, ln1), (ln2_sb, ln2)):
                sp.dma_start(dst[:], src).then_inc(small_ld, 16)
            load_v(0)
            sp.dma_start(raw_wo[:], wo.rearrange("(ot p) j -> p ot j", p=P)).then_inc(woa_ld, 16)
            sp.dma_start(a_sb[:], a4.rearrange("(ot p) r -> p ot r", p=P)).then_inc(woa_ld, 16)
            sp.dma_start(raw_wv[:], wv.rearrange("(jt p) d -> p jt d", p=P)).then_inc(woa_ld, 16)
            sp.dma_start(raw_wq[:], wqT.rearrange("(db p) j -> p db j", p=P)).then_inc(w_ld, 16)
            sp.dma_start(raw_wk[:], wkT.rearrange("(db p) j -> p db j", p=P)).then_inc(w_ld, 16)
            sp.wait_ge(const_rdy, 2)
            for row in (0, 2 * R, 4 * R):
                sp.dma_start(raw_b[row:row + R, :], b_mod).then_inc(b_ld, 16)
            for f in range(2):
                load_gu(f)
                load_d(f)

            def batch(b, last):
                def stack(g):
                    for i, (st, low, second) in enumerate(((q_st, 32, 64), (k_st, 64, 32))):
                        if g >= STAGED:
                            sp.wait_ge(qk_lo, b * 2 * G + 2 * g + i + 1)
                            if g >= 3:
                                sp.wait_ge(st_ps, 2 * (b * STEPS + 6 * (g - 2)))
                            for j in range(4):
                                sp.dma_start(f32(st[g % 3][low:low + 32, j, :]), f32(qk_lo4[i][quad(j), :])).then_inc(rep_ld[g], 16)
                        sp.wait_ge(qk_hi, b * 8 * G + 8 * g + 4 * i + 4)
                        sp.dma_start(f32(st[g % 3][second:second + 32, :, :]), f32(st[g % 3][0:32, :, :])).then_inc(rep_ld[g], 16)

                def maxima(g):
                    sp.wait_ge(nmrow_rdy, b * G + g + 1)
                    for c in range(2):
                        sp.dma_start(f32(q_st[g % 3][96 + c:97 + c, :, :]), f32(nmrow[4 * c:4 * c + 4, :])).then_inc(nm_ld[g], 16)

                stack(0)
                stack(1)
                maxima(0)
                stack(2)
                maxima(1)
                stack(3)
                maxima(2)
                maxima(3)
                if not last:
                    sp.wait_ge(pv_ps, (b + 1) * G)
                    load_x(b + 1)
                for f in (2, 3):
                    sp.wait_ge(gu_lo, b * NF + f - 1)
                    load_gu(f)
                sp.wait_ge(wd_lo, b * NF + 1)
                load_d(2)
                if not last:
                    load_v(b + 1)
                for f in range(NF):
                    if f + 4 < NF + 2 and not (last and f + 4 >= NF):
                        sp.wait_ge(gu_lo, b * NF + f + 3)
                        load_gu((f + 4) % NF)
                    if f + 3 < NF + 2 and not (last and f + 3 >= NF):
                        sp.wait_ge(wd_lo, b * NF + f + 2)
                        load_d((f + 3) % NF)
                for tb in range(TB):
                    sp.wait_ge(fin_rdy, b * TB + tb + 1)
                    sp.dma_start(out[bass.ds(b, 1), blk(tb), :].rearrange("o p d -> (o p) d"), base[:, tb, :]).then_inc(base_free, 16)

            with sp.Fori(0, NB - 1) as b:
                batch(b, False)
            batch(NB - 1, True)
            sp.wait_ge(base_free, 64 * (NB + 1))

        @block.gpsimd
        def _(pool):
            pool.memset(raw_b[:], 0.0).then_inc(const_rdy, 1)
            pool.memset(ident[:], 0.0).then_inc(pool_own, 1)
            pool.memset(mask_qk[:], 0.0).then_inc(pool_own, 1)
            pool.memset(mask_kq[:], 0.0).then_inc(pool_own, 1)
            pool.memset(minus_half[:], -0.5).then_inc(const_rdy, 1)
            pool.wait_ge(pool_own, 3)
            pool.affine_select(out=ident[:], in_=ident[:], compare_op=ALU.not_equal, fill=1.0, base=0,
                               pattern=[[-1, P]], channel_multiplier=1).then_inc(pool_own, 1)
            pool.affine_select(out=mask_qk[:], in_=mask_qk[:], compare_op=ALU.is_ge, fill=MASKED, base=0,
                               pattern=[[-1, P]], channel_multiplier=1).then_inc(const_rdy, 1)
            pool.affine_select(out=mask_kq[:], in_=mask_kq[:], compare_op=ALU.is_ge, fill=MASKED, base=0,
                               pattern=[[1, P]], channel_multiplier=-1).then_inc(const_rdy, 1)
            pool.iota(steps[:], [[1, T]], base=0, channel_multiplier=0,
                      allow_small_or_imprecise_dtypes=True).then_inc(const_rdy, 1)
            pool.wait_ge(pool_own, 4)
            pool.tensor_copy(identb[:], ident[:]).then_inc(const_rdy, 1)
            pool.memset(v_aug[:], 0.0).then_inc(pool_own, 1)
            pool.wait_ge(pool_own, 5)
            pool.memset(v_aug[:, :, :, R:R + 1], 1.0).then_inc(const_rdy, 1)
            pool.memset(tcols[:], 0.0).then_inc(const_rdy, 1)
            pool.memset(woa[:], 0.0).then_inc(const_rdy, 1)

            def rstd_of_x(n):
                pool.wait_ge(stats1, n + 1)
                pool.tensor_tensor(rstd[:], var_eps[:], minus_half[:], ALU.pow).then_inc(rstd1, 1)

            def weigh_values(n, cb, first=False):
                if cb == 0:
                    pool.wait_ge(v_ld, 16 * (n + 1))
                pool.wait_ge(kexp_rdy, n * DB + cb + 1)
                pool.tensor_tensor(kv_of(cb, first), k_of(cb, first), vT[:, cb, :], ALU.mult).then_inc(kv_rdy, 1)

            def product(n, cb, first=False):
                pool.wait_ge(recip_rdy, n * DB + cb + 1)
                pool.tensor_tensor(yT[:, cb, :], kv_of(cb, first), k_of(cb, first), ALU.mult).then_inc(yT_rdy, 1)

            def scales_of_x1(n):
                pool.wait_ge(stats2, n + 1)
                pool.tensor_tensor(hn_scale[:], var_both[:], minus_half[:], ALU.pow).then_inc(scale2, 1)
                pool.tensor_tensor(rstdb[:], var_epsb[:], minus_half[:], ALU.pow).then_inc(rstd2, 1)

            def low_gu(b, f):
                pool.wait_ge(gu_hi, b * NF + f + 1)
                pool.tensor_tensor(gu_s[f % 2][1][:], raw_gu[f % 2][:], f32(gu_s[f % 2][0][:]), ALU.subtract).then_inc(gu_lo, 1)

            def low_d(b, f):
                pool.wait_ge(wd_hi, b * NF + f + 1)
                pool.tensor_tensor(wd_s[f % 2][1][:], raw_d[f % 2][:], f32(wd_s[f % 2][0][:]), ALU.subtract).then_inc(wd_lo, 1)

            rstd_of_x(0)
            pool.wait_ge(rstd1, 1)
            for i in range(3):
                pool.memset(f32(k_st[i][96:98, :, :]), 1.0).then_inc(ones_rdy, 1)
            pool.wait_ge(ones_rdy, 3)
            for cb in range(DB):
                weigh_values(0, cb, True)
            def low_qk(i, db):
                raw, dst = ((raw_wq, wq_s), (raw_wk, wk_s))[i]
                pool.wait_ge(wsplit_hi, DB * i + db + 1)
                pool.tensor_tensor(dst[1][:, db, :], raw[:, db, :], f32(dst[0][:, db, :]), ALU.subtract).then_inc(wsplit_lo, 1)

            product(0, 0, True)
            product(0, 1, True)
            for i, db in ((0, 0), (0, 1), (1, 0)):
                low_qk(i, db)
            product(0, 2, True)
            for i, db in ((0, 2), (0, 3), (1, 1)):
                low_qk(i, db)
            product(0, 3, True)
            for i, db in ((1, 2), (1, 3)):
                low_qk(i, db)
            scales_of_x1(0)
            pool.wait_ge(wsplit_hi, 2 * DB + 1)
            pool.wait_ge(rstd2, 1)
            pool.tensor_tensor(b_s[4 * R:5 * R, :], raw_b[4 * R:5 * R, :], f32(b_s[4 * R:5 * R, :]), ALU.subtract).then_inc(base_free, 64)
            pool.wait_ge(base_free, 64)

            def batch(b, last):
                low_gu(b, 0)
                low_gu(b, 1)
                low_d(b, 0)
                for f in range(NF):
                    if f + 2 < NF:
                        low_gu(b, f + 2)
                    if f + 1 < NF:
                        low_d(b, f + 1)
                    if not last:
                        if f == 0:
                            rstd_of_x(b + 1)
                        for cb in range(DB):
                            if f == KEYS_AT[cb]:
                                weigh_values(b + 1, cb)
                            if f == RECIP_AT[cb][1]:
                                product(b + 1, cb)
                        if f == NORM2_AT:
                            scales_of_x1(b + 1)

            with pool.Fori(0, NB - 1) as b:
                batch(b, False)
            batch(NB - 1, True)

        @block.scalar
        def _(act):
            act.wait_ge(prep_rdy, 1)
            act.activation(decay[:], w_minus[:], ACT.Exp)
            act.activation(rho[:], bonus[:], ACT.Exp, scale=-1.0)
            act.activation(gate_t[:], gates_sb[:], ACT.Tanh).then_inc(decay_rdy, 1)

            def kexp_step(n, cb, first=False):
                act.wait_ge(kt_rdy, n * DB + cb + 1)
                act.activation(k_of(cb, first), k_of(cb, first), ACT.Exp, bias=shift[:, cb:cb + 1]).then_inc(kexp_rdy, 1)

            for cb in range(DB):
                kexp_step(0, cb, True)
            act.wait_ge(const_rdy, 9)
            act.wait_ge(woa_ps, 1)
            for j in range(4):
                op = act.activation(woa[quad(j), :, R * j:R * j + R], ps[quad(j), 0, 0:DB * R].rearrange("p (t r) -> p t r", r=R), ACT.Copy)
            op.then_inc(woa_sb, 1)
            act.wait_ge(w_ld, 32)
            for raw in (raw_wq, raw_wk):
                for db in range(DB):
                    act.activation(raw[:, db, :], raw[:, db, :], ACT.Copy, scale=ln1_sb[:, db:db + 1]).then_inc(wscaled, 1)
            for i, (raw, dst) in enumerate(((raw_wq, wq_s), (raw_wk, wk_s))):
                for db in range(DB):
                    act.wait_ge(wscaled, DB * i + db + 1)
                    act.activation(dst[0][:, db, :], raw[:, db, :], ACT.Copy).then_inc(wsplit_hi, 1)
            act.wait_ge(b_ld, 48)
            act.activation(b_s[:], raw_b[:], ACT.Copy).then_inc(wsplit_hi, 1)
            act.wait_ge(ga_ps, 1)
            for db in range(DB):
                act.activation(ga_s[0][:, db, 0:H * R], ps[:, 2 + db // 2, 256 * (db % 2):256 * (db % 2) + 256], ACT.Copy,
                               scale=ln1_sb[:, db:db + 1])
                act.activation(ga_s[0][:, db, H * R:GA], a_sb[:, db, :], ACT.Copy, scale=ln2_sb[:, db:db + 1]).then_inc(ga_hi, 1)

            def normed(n):
                for db in range(DB):
                    act.wait_ge(hnT_ps, n * DB + db + 1)
                    act.activation(hn_s[0][:, db, :], ps[:, HB[db], :], ACT.Copy).then_inc(hn_hi, 1)
                for db in H_ORDER:
                    act.wait_ge(hn_lo, n * DB + db + 1)
                    act.activation(h_s[0][:, db, :], ps[:, HB[db], :], ACT.Copy, scale=ln2_sb[:, db:db + 1]).then_inc(h_hi, 1)

            normed(0)

            def split_gu(b, f):
                act.wait_ge(gu_ld[f % 2], (b * NF + f - f % 2) * 8 + 16)
                if f >= 2:
                    act.wait_ge(up_ps, b * NF + f - 1)
                act.activation(gu_s[f % 2][0][:], raw_gu[f % 2][:], ACT.Copy).then_inc(gu_hi, 1)

            def split_d(b, f):
                act.wait_ge(d_ld[f % 2], (b * NF + f - f % 2) * 8 + 16)
                if f >= 2:
                    act.wait_ge(down_ps, b * (NF - 1) + f - 1)
                act.activation(wd_s[f % 2][0][:], raw_d[f % 2][:], ACT.Copy).then_inc(wd_hi, 1)

            def batch(b, last):
                def make_base():
                    act.wait_ge(base_scale, b + 1)
                    act.wait_ge(base_free, 64 * (b + 1))
                    for tb in range(TB):
                        op = act.activation(base[:, tb, :], x_sb[:, tb, :], ACT.Identity, scale=base_mul[:, tb:tb + 1], bias=base_add[:, tb:tb + 1])
                    op.then_inc(base_rdy, 1)

                def minus_max_rows(g):
                    act.wait_ge(nm_ps, b * G + g + 1)
                    if g >= 1:
                        act.wait_ge(nm_ld[g - 1], 32 * (b + 1))
                    act.activation(nmrow[:], ps[0:8, TPB, :], ACT.Copy).then_inc(nmrow_rdy, 1)

                def qk_stage_hi(g, i):
                    act.wait_ge(qk_ps, b * 2 * G + 2 * g + i + 1)
                    act.wait_ge(qk_lo, b * 2 * G + 2 * g + i)
                    act.wait_ge(qk_hi, b * 8 * G + 8 * g + 4 * i)
                    act.activation(qk_hi4[:], ps[:, 4 + i, :], ACT.Copy).then_inc(qk_stage, 1)

                def qk_round(g, i):
                    act.wait_ge(qk_ps, b * 2 * G + 2 * g + i + 1)
                    for j in range(4):
                        act.activation((q_st, k_st)[i][g][0:32, j, :], ps[quad(j), 4 + i, :], ACT.Copy).then_inc(qk_hi, 1)

                def q_copy(g):
                    act.wait_ge(qk_stage, b * 2 * (G - STAGED) + 2 * (g - STAGED) + 1)
                    if g >= 3:
                        act.wait_ge(st_ps, 2 * (b * STEPS + 6 * (g - 2)))
                    for j in range(4):
                        act.activation(q_st[g % 3][0:32, j, :], f32(qk_hi4[quad(j), :]), ACT.Copy).then_inc(qk_hi, 1)

                def values(tb):
                    act.wait_ge(va_ps, b * TB + tb + 1)
                    bank = VALUE_BANK[tb]
                    act.activation(v_aug[:, tb, :, 0:R], ps[:, bank, 0:H * R].rearrange("p (h r) -> p h r", r=R), ACT.Copy)
                    act.activation(h_a[:, tb, :], ps[:, bank, H * R:GA], ACT.Copy).then_inc(va_sb, 1)

                def exps(m):
                    g, s, pr = m // 6, m % 6 // 2, m % 2
                    if m == 6:
                        act.wait_ge(base_rdy, b + 1)
                    if m % 6 == 0 and g >= 2:
                        act.wait_ge(pv_ps, b * G + g - 1)
                    at, width = ST_E[s]
                    for i in range(2):
                        act.wait_ge(st_ps, 2 * (b * STEPS + m) + i + 1)
                        act.activation(e_row[g % 2][:, 2 * pr + i, at:at + width], ps[:, st_bank(m) + i, 0:width],
                                       ACT.Exp, scale=SM_SCALE).then_inc(exp_rdy, 1)

                def weighted(g):
                    act.wait_ge(pv_ps, b * G + g + 1)
                    if g >= 1:
                        act.wait_ge(pvT_ps, b * G + g)
                    act.activation(pvs[:], ps[:, 6, :], ACT.Copy).then_inc(pvs_rdy, 1)

                qk_round(0, 0)
                qk_round(0, 1)
                values(0)
                values(1)
                for n in range(STEPS + LAG):
                    if n == BASE_AT:
                        make_base()
                    if n % 6 == 0 and 6 <= n <= STEPS:
                        minus_max_rows(n // 6 - 1)
                    m = n - LAG
                    if m >= 0:
                        exps(m)
                    if n in ROUND_AT:
                        qk_round(1, ROUND_AT.index(n))
                    for g, at in STAGE_AT.items():
                        if n in at:
                            qk_stage_hi(g, at.index(n))
                    for g, at in COPY_AT.items():
                        if n == at[0]:
                            q_copy(g)
                    for tb, at in VALUE_AT.items():
                        if n == at + 1:
                            values(tb)
                    if m >= 6 and m % 6 == 0:
                        weighted(m // 6 - 1)
                    if n in SPLIT_AT:
                        split_gu(b, SPLIT_AT.index(n))
                weighted(G - 1)
                split_d(b, 0)
                act.wait_ge(modsum_rdy, b + 1)
                act.activation(modt[:], modsum[:], ACT.Tanh).then_inc(modt_rdy, 1)
                for f in range(NF):
                    act.wait_ge(gate_ps, b * NF + f + 1)
                    act.activation(th[:], ps[:, 4 + (2 * f) % 3, :], ACT.Tanh, scale=0.5).then_inc(th_rdy, 1)
                    act.wait_ge(prod_rdy, b * NF + f + 1)
                    if f >= 2:
                        act.wait_ge(down_ps, b * (NF - 1) + f - 1)
                    act.activation(act_s[f % 2][0][:], prod[:], ACT.Copy).then_inc(act_hi, 1)
                    if f + 2 < NF:
                        split_gu(b, f + 2)
                    if f + 1 < NF:
                        split_d(b, f + 1)
                    if not last and f in KEYS_AT:
                        kexp_step(b + 1, KEYS_AT.index(f))
                if not last:
                    normed(b + 1)

            with act.Fori(0, NB - 1) as b:
                batch(b, False)
            batch(NB - 1, True)

        @block.vector
        def _(dve):
            own = {"base": 0, "n": 0}

            def mine(op):
                own["n"] += 1
                op.then_inc(dve_own, 1)

            def settled():
                dve.wait_ge(dve_own, own["base"] + own["n"])

            def moments(stats, mean, var):
                settled()
                mine(dve.tensor_tensor(half_diff[:], stats[:, :, 1], stats[:, :, 4], ALU.subtract))
                mine(dve.tensor_tensor(mean[:], stats[:, :, 1], stats[:, :, 4], ALU.add))
                mine(dve.tensor_tensor(var[:], stats[:, :, 2], stats[:, :, 5], ALU.add))
                settled()
                mine(dve.scalar_tensor_tensor(half_diff[:], half_diff[:], 0.25, half_diff[:], ALU.mult, ALU.mult))
                mine(dve.tensor_scalar(mean[:], mean[:], 0.5, None, ALU.mult))
                settled()
                mine(dve.scalar_tensor_tensor(var[:], var[:], 1.0 / D, half_diff[:], ALU.mult, ALU.add))
                settled()

            def norm1(n):
                for tb in range(TB):
                    dve.wait_ge(x_ld[tb], 16 * (n + 1))
                    op = dve.bn_stats(bn6[:, tb, :], x_sb[:, tb, :])
                mine(op)
                moments(bn6, mean, var)
                dve.tensor_scalar(var_eps[:], var[:], LN_EPS, None, ALU.add).then_inc(stats1, 1)

            def norm1_apply(n, first):
                dve.wait_ge(rstd1, n + 1)
                if not first:
                    dve.wait_ge(hnT_ps, n * DB)
                for tb in range(TB):
                    op = dve.tensor_scalar(norm[:, tb, :], x_sb[:, tb, :], mean[:, tb:tb + 1], rstd[:, tb:tb + 1],
                                           ALU.subtract, ALU.mult)
                op.then_inc(xn_rdy, 1)

            def keys(n, cb, first, bank=TPB):
                dve.wait_ge(xnT_ps, n * DB + cb + 1)
                if cb == 0 and not first:
                    dve.wait_ge(pv_ps, n * G)
                if cb >= 2 and not first:
                    dve.wait_ge(yT_rdy, n * DB + cb - 1)
                dve.scalar_tensor_tensor(k_of(cb, first), steps[:], neg_wp[:, cb:cb + 1], ps[:, bank, :],
                                         ALU.mult, ALU.add).then_inc(kt_rdy, 1)

            def scans(n, cb, first=False):
                if cb == 0:
                    dve.memset(p_run[:, 0:1], 0.0)
                    dve.memset(q_run[:, 0:1], 0.0)
                a = decay[:, cb:cb + 1].broadcast_to([P, T])
                dve.wait_ge(kv_rdy, n * DB + cb + 1)
                k, kv_ = k_of(cb, first), kv_of(cb, first)
                dve.tensor_tensor_scan(q_run[:, 1:T + 1], a, k, 0.0, ALU.mult, ALU.add)
                mine(dve.tensor_tensor_scan(p_run[:, 1:T + 1], a, kv_, 0.0, ALU.mult, ALU.add))
                settled()
                dve.scalar_tensor_tensor(k, q_run[:, 0:T], rho[:, cb:cb + 1], k, ALU.mult, ALU.add)
                mine(dve.scalar_tensor_tensor(kv_, p_run[:, 0:T], rho[:, cb:cb + 1], kv_, ALU.mult, ALU.add))

            def recips(n, cb, half=None, first=False):
                settled()
                at = slice(0, T) if half is None else slice(half * T // 2, (half + 1) * T // 2)
                op = dve.reciprocal(k_of(cb, first)[:, at], k_of(cb, first)[:, at])
                if half == 0:
                    mine(op)
                else:
                    op.then_inc(recip_rdy, 1)

            def residual1(n, tb, bank=TPB):
                dve.wait_ge(yT_ps, n * TB + tb + 1)
                dve.scalar_tensor_tensor(x_sb[:, tb, :], ps[:, bank, :], gate_t[:, 0:1], x_sb[:, tb, :],
                                         ALU.mult, ALU.add).then_inc(x1_rdy, 1)

            def x1_stats(n, tb):
                dve.wait_ge(x1_rdy, n * TB + tb + 1)
                mine(dve.bn_stats(bn6b[:, tb, :], x_sb[:, tb, :]))

            def norm2(n):
                moments(bn6b, meanb, varb)
                mine(dve.tensor_scalar(var_epsb[:], varb[:], LN_EPS, None, ALU.add))
                settled()
                dve.scalar_tensor_tensor(var_both[:], var_epsb[:], RMS_EPS, varb[:], ALU.mult, ALU.add).then_inc(stats2, 1)
                dve.wait_ge(scale2, n + 1)
                dve.wait_ge(xnT_ps, (n + 1) * DB)
                for tb in range(TB):
                    op = dve.tensor_scalar(norm[:, tb, :], x_sb[:, tb, :], meanb[:, tb:tb + 1], hn_scale[:, tb:tb + 1],
                                           ALU.subtract, ALU.mult)
                op.then_inc(hn_rdy, 1)
                dve.wait_ge(rstd2, n + 1)
                mine(dve.tensor_scalar(gr[:], rstdb[:], gate_t[:, 1:2], None, ALU.mult))
                settled()
                dve.tensor_scalar(base_mul[:], gr[:], 1.0, None, ALU.add)
                dve.scalar_tensor_tensor(base_add[:], meanb[:], -1.0, gr[:], ALU.mult, ALU.mult).then_inc(base_scale, 1)

            norm1(0)
            dve.wait_ge(small_ld, 80)
            mine(dve.tensor_scalar(neg_wp[:], w_sb[:], 0.0, -1.0, ALU.max, ALU.mult))
            mine(dve.tensor_scalar(w_minus[:], w_sb[:], 0.0, None, ALU.min))
            settled()
            mine(dve.tensor_tensor(bonus[:], u_sb[:], neg_wp[:], ALU.subtract))
            settled()
            mine(dve.tensor_scalar(bonus[:], bonus[:], BONUS_LOW, None, ALU.max))
            settled()
            dve.tensor_scalar(shift[:], bonus[:], 0.0, SHIFT_LOW, ALU.min, ALU.max).then_inc(prep_rdy, 1)
            norm1_apply(0, True)
            dve.wait_ge(decay_rdy, 1)
            dve.tensor_scalar(half_gate[:], gate_t[:, 1:2], 0.5, None, ALU.mult)
            dve.wait_ge(const_rdy, 5)
            for cb in range(DB):
                keys(0, cb, True, 4 + cb)
            for cb in range(DB):
                scans(0, cb, True)
                recips(0, cb, None, True)
            dve.wait_ge(ga_hi, DB)
            for db in range(DB):
                dve.scalar_tensor_tensor(ga_s[1][:, db, 0:H * R], ps[:, 2 + db // 2, 256 * (db % 2):256 * (db % 2) + 256],
                                         ln1_sb[:, db:db + 1], f32(ga_s[0][:, db, 0:H * R]), ALU.mult, ALU.subtract)
                dve.scalar_tensor_tensor(ga_s[1][:, db, H * R:GA], a_sb[:, db, :], ln2_sb[:, db:db + 1],
                                         f32(ga_s[0][:, db, H * R:GA]), ALU.mult, ALU.subtract).then_inc(ga_lo, 1)
            for tb in range(TB):
                residual1(0, tb, 4 + tb)
                if tb >= 1:
                    x1_stats(0, tb - 1)
            x1_stats(0, TB - 1)
            norm2(0)
            own_prologue = own["n"]

            def normed(n):
                for db in range(DB):
                    dve.wait_ge(hn_hi, n * DB + db + 1)
                    dve.tensor_tensor(hn_s[1][:, db, :], ps[:, HB[db], :], f32(hn_s[0][:, db, :]), ALU.subtract).then_inc(hn_lo, 1)
                for i, db in enumerate(H_ORDER):
                    dve.wait_ge(h_hi, n * DB + i + 1)
                    dve.scalar_tensor_tensor(h_s[1][:, db, :], ps[:, HB[db], :], ln2_sb[:, db:db + 1], f32(h_s[0][:, db, :]),
                                             ALU.mult, ALU.subtract).then_inc(h_lo, 1)

            def finish(b):
                for tb in range(TB):
                    dve.wait_ge(mlp_ps, b * TB + tb + 1)
                    dve.scalar_tensor_tensor(base[:, tb, :], ps[:, tb, :], half_gate[:], base[:, tb, :],
                                             ALU.mult, ALU.add).then_inc(fin_rdy, 1)

            normed(0)

            def batch(b, last):
                own["base"], own["n"] = own_prologue + b * DVE_OWN_PER_BATCH, 0

                def qk_low(g, i, heads=range(4)):
                    st, at = ((q_st, 32), (k_st, 64))[i]
                    for j in heads:
                        dve.wait_ge(qk_hi, b * 8 * G + 8 * g + 4 * i + j + 1)
                        op = dve.tensor_tensor(st[g][at:at + 32, j, :], ps[quad(j), 4 + i, :], f32(st[g][0:32, j, :]), ALU.subtract)
                    if 3 in heads:
                        op.then_inc(qk_lo, 1)

                def qk_low4(g, i):
                    dve.wait_ge(qk_stage, b * 2 * (G - STAGED) + 2 * (g - STAGED) + i + 1)
                    if g > STAGED:
                        dve.wait_ge(rep_ld[g - 1], 160 * (b + 1))
                    dve.tensor_tensor(qk_lo4[i][:], ps[:, 4 + i, :], f32(qk_hi4[:]), ALU.subtract).then_inc(qk_lo, 1)

                def k_copy(g):
                    dve.wait_ge(qk_stage, b * 2 * (G - STAGED) + 2 * (g - STAGED) + 2)
                    if g >= 3:
                        dve.wait_ge(st_ps, 2 * (b * STEPS + 6 * (g - 2)))
                    for j in range(4):
                        dve.tensor_copy(k_st[g % 3][0:32, j, :], f32(qk_hi4[quad(j), :])).then_inc(qk_hi, 1)

                def maxima(n):
                    g, s, pr = n // 6, n % 6 // 2, n % 2
                    if n % 6 == 0 and g >= 1:
                        dve.wait_ge(nmc_rdy, b * G + g)
                    for i in range(2):
                        j = 2 * pr + i
                        dve.wait_ge(s_ps, 2 * (b * STEPS + n) + i + 1)
                        for at, qb in S_STEPS[s]:
                            op = dve.reduce_max(mx[:, qb, j:j + 1], ps[:, s_bank(n) + i, at:at + (qb + 1) * P], AX.X)
                        op.then_inc(smax_rdy, 1)
                        for c in range(8):
                            if LOW_HALF[c] == 2 * n + i:
                                qk_low(1, c // 4, (c % 4,))

                def minus_max(g):
                    dve.wait_ge(smax_rdy, 2 * (b * STEPS + 6 * g + 6))
                    if g >= 1:
                        dve.wait_ge(nm_ps, b * G + g)
                    mine(dve.tensor_scalar(nmc[:, :, 0:4].bitcast(F32R), mx[:], -1.0, None, ALU.mult))
                    settled()
                    dve.scalar_tensor_tensor(nmc[:, :, 4:8], mx[:], -1.0, nmc[:, :, 0:4], ALU.mult, ALU.subtract).then_inc(nmc_rdy, 1)

                def weighted(g):
                    dve.wait_ge(pvT_ps, b * G + g + 1)
                    pvT = ps[:, TPB, :].rearrange("p (q j c) -> p q j c", q=TB, j=4)
                    mine(dve.reciprocal(rl[:], pvT[:, :, :, R]))
                    settled()
                    for qb in range(TB):
                        op = dve.tensor_tensor(pvn[g % 2][:, qb, 0:4, :], pvT[:, qb, :, 0:R], rl[:, qb, :].unsqueeze(2).broadcast_to([P, 4, R]), ALU.mult)
                    op.then_inc(pvT_used, 1)
                    dve.wait_ge(pvT_used, b * G + g + 1)
                    terms = pvn[g % 2][:, :, 0:4 if g == 0 else 5, :].rearrange("p q j r -> p q r j")
                    if g < G - 1:
                        mine(dve.reduce_sum(pvn[(g + 1) % 2][:, :, 4, :], terms, AX.X))
                    else:
                        settled()
                        dve.reduce_sum(modsum[:], terms, AX.X).then_inc(modsum_rdy, 1)

                qk_low(0, 0)
                qk_low(0, 1)
                for n in range(STEPS + LAG):
                    if n < STEPS:
                        maxima(n)
                    if n % 6 == 5 and n < STEPS:
                        minus_max(n // 6)
                    for g, at in LOW_AT.items():
                        if n in at:
                            qk_low4(g, at.index(n))
                        if n == COPY_AT[g][1]:
                            k_copy(g)
                    if n >= NORM_LAG and (n - NORM_LAG) % 6 == 0:
                        weighted((n - NORM_LAG) // 6)
                weighted(G - 1)
                dve.wait_ge(modt_rdy, b + 1)
                mine(dve.scalar_tensor_tensor(t_mod[:], modt[:], MOD_SCALE, h_a[:], ALU.mult, ALU.mult))
                settled()
                dve.tensor_copy(tcols[:, :, 0:R].bitcast(F32R), t_mod[:])
                mine(dve.tensor_copy(tcols[:, :, 4 * R:5 * R].bitcast(F32R), t_mod[:]))
                settled()
                dve.tensor_tensor(tcols[:, :, 2 * R:3 * R], t_mod[:], tcols[:, :, 0:R], ALU.subtract).then_inc(t_rdy, 1)
                dve.wait_ge(tT_ps, b + 1)
                dve.tensor_copy(t_s[:], ps[0:5 * R, TPB, :]).then_inc(tT_rdy, 1)

                for f in range(NF):
                    dve.wait_ge(th_rdy, b * NF + f + 1)
                    if f >= 1:
                        dve.wait_ge(prod_rdy, b * NF + f)
                    dve.scalar_tensor_tensor(gsil[:], th[:], 1.0, ps[:, 4 + (2 * f) % 3, :], ALU.add, ALU.mult).then_inc(gsil_rdy, 1)
                    dve.wait_ge(up_ps, b * NF + f + 1)
                    dve.wait_ge(gsil_rdy, b * NF + f + 1)
                    if f >= 1:
                        dve.wait_ge(act_lo, b * NF + f)
                    dve.tensor_tensor(prod[:], gsil[:], ps[:, 4 + (2 * f + 1) % 3, :], ALU.mult).then_inc(prod_rdy, 1)
                    dve.wait_ge(act_hi, b * NF + f + 1)
                    dve.tensor_tensor(act_s[f % 2][1][:], prod[:], f32(act_s[f % 2][0][:]), ALU.subtract).then_inc(act_lo, 1)
                    if not last:
                        n = b + 1
                        if f == 0:
                            norm1(n)
                        if f == 1:
                            norm1_apply(n, False)
                        for cb in range(DB):
                            if f == RECIP_AT[cb][1] and RECIP_AT[cb][0] < f:
                                recips(n, cb, 1)
                        for cb in range(DB):
                            if f == SCANS_AT[cb]:
                                if f == KEYS_AT[(cb + 1) % DB]:
                                    keys(n, cb + 1, False)
                                scans(n, cb)
                        for cb in range(DB):
                            if f == RECIP_AT[cb][0]:
                                recips(n, cb, 0 if RECIP_AT[cb][1] > f else None)
                        if f in KEYS_AT and f not in SCANS_AT:
                            keys(n, KEYS_AT.index(f), False)
                        if Y_AT <= f < Y_AT + TB:
                            residual1(n, f - Y_AT)
                            x1_stats(n, f - Y_AT)
                        if f == NORM2_AT:
                            norm2(n)
                if not last:
                    normed(b + 1)
                finish(b)
                assert last or own["n"] == DVE_OWN_PER_BATCH, own["n"]

            with dve.Fori(0, NB - 1) as b:
                batch(b, False)
            batch(NB - 1, True)

        @block.tensor
        def _(pe):
            def split_matmul(dst, w_hi, w_lo, m_hi, m_lo, start, stop):
                pe.matmul(dst, w_hi, m_hi, start=start, stop=False)
                pe.matmul(dst, w_hi, m_lo, start=False, stop=False)
                return pe.matmul(dst, w_lo, m_hi, start=False, stop=stop)

            def keys_T(n, cb, bank=TPB, shared=True):
                pe.wait_ge(xn_rdy, n + 1)
                if cb >= 1 and shared:
                    pe.wait_ge(kt_rdy, n * DB + cb)
                for tb in range(TB):
                    op = pe.transpose(ps[:, bank, blk(tb)], norm[:, tb, blk(cb)], ident[:])
                op.then_inc(xnT_ps, 1)

            def rows_y(n, tb, bank=TPB, shared=True):
                pe.wait_ge(yT_rdy, (n + 1) * DB)
                if tb >= 1 and shared:
                    pe.wait_ge(x1_rdy, n * TB + tb)
                for cb in range(DB):
                    op = pe.transpose(ps[:, bank, blk(cb)], yT[:, cb, blk(tb)], ident[:])
                op.then_inc(yT_ps, 1)

            def normed_T(n, db):
                pe.wait_ge(hn_rdy, n + 1)
                for tb in range(TB):
                    op = pe.transpose(ps[:, HB[db], blk(tb)], norm[:, tb, blk(db)], ident[:])
                op.then_inc(hnT_ps, 1)

            pe.wait_ge(const_rdy, 6)
            for cb in range(DB):
                keys_T(0, cb, 4 + cb, False)
            pe.wait_ge(woa_ld, 48)
            for jt in range(DB):
                for ot in range(DB):
                    op = pe.matmul(ps[:, 0, R * jt:R * jt + R], raw_wo[:, ot, blk(jt)], a_sb[:, ot, :],
                                   start=ot == 0, stop=ot == DB - 1)
            op.then_inc(woa_ps, 1)
            pe.wait_ge(woa_sb, 1)
            for db in range(DB):
                for jt in range(DB):
                    at = 256 * (db % 2) + 4 * R * jt
                    op = pe.matmul(ps[:, 2 + db // 2, at:at + 4 * R], raw_wv[:, jt, blk(db)], woa[:, jt, :], start=True, stop=True)
            op.then_inc(ga_ps, 1)
            for tb in range(TB):
                rows_y(0, tb, 4 + tb, False)
            for db in range(DB):
                normed_T(0, db)
            pe.wait_ge(wsplit_lo, 2 * DB)
            pe.wait_ge(ones_rdy, 3)
            pe.wait_ge(const_rdy, 8)

            def batch(b, last):
                def project(g, i, dbs=range(DB)):
                    w = (wq_s, wk_s)[i]
                    if g == 0:
                        pe.wait_ge(h_lo, b * DB + i + 1)
                    elif 0 in dbs:
                        pe.wait_ge(qk_lo, b * 2 * G + 2 * (g - 1) + i + 1)
                    for db in dbs:
                        op = split_matmul(ps[:, 4 + i, :], w[0][:, db, blk(g)], w[1][:, db, blk(g)], hn_s[0][:, db, :], hn_s[1][:, db, :],
                                          db == 0, db == DB - 1)
                    if DB - 1 in dbs:
                        op.then_inc(qk_ps, 1)

                def values(tb):
                    if tb < 2:
                        pe.wait_ge(h_lo, b * DB + 2 + tb + 1)
                    else:
                        pe.wait_ge(va_sb, b * TB + 2)
                    for db in range(DB):
                        op = split_matmul(ps[:, VALUE_BANK[tb], 0:GA], hn_s[0][:, db, blk(tb)], hn_s[1][:, db, blk(tb)],
                                          ga_s[0][:, db, :], ga_s[1][:, db, :], db == 0, db == DB - 1)
                    op.then_inc(va_ps, 1)

                def scores(n):
                    g, s, pr = n // 6, n % 6 // 2, n % 2
                    if n % 6 == 0:
                        pe.wait_ge(rep_ld[g], (32 if g < STAGED else 160) * (b + 1))
                        pe.wait_ge(qk_lo, b * 2 * G + 2 * g + 2)
                    for i in range(2):
                        j = 2 * pr + i
                        before = 2 if n <= LAG else 1
                        if n >= before:
                            pe.wait_ge(smax_rdy, 2 * (b * STEPS + n - before) + i + 1)
                        for at, qb in S_STEPS[s]:
                            w = (qb + 1) * P
                            pe.matmul(ps[:, s_bank(n) + i, at:at + w], q_st[g % 3][0:96, j, blk(qb)], k_st[g % 3][0:96, j, 0:w], start=True, stop=False)
                            op = pe.matmul(ps[:, s_bank(n) + i, at + w - P:at + w], identb[:], mask_qk[:], start=False, stop=True)
                        op.then_inc(s_ps, 1)

                def scores_T(m):
                    g, s, pr = m // 6, m % 6 // 2, m % 2
                    if m % 6 == 0:
                        pe.wait_ge(nm_ld[g], 32 * (b + 1))
                    if m == 0:
                        pe.wait_ge(smax_rdy, 2 * (b * STEPS + LAG))
                    elif m == TWO_PAIRS:
                        pe.wait_ge(smax_rdy, 2 * (b + 1) * STEPS)
                    before = 1 if m < TWO_PAIRS else 2
                    for i in range(2):
                        if m >= 1 and m != TWO_PAIRS:
                            pe.wait_ge(exp_rdy, 2 * (b * STEPS + m - before) + i + 1)
                        for at, kb in ST_STEPS[s]:
                            w = T - kb * P
                            pe.matmul(ps[:, st_bank(m) + i, at:at + w], k_st[g % 3][0:98, 2 * pr + i, blk(kb)],
                                      q_st[g % 3][0:98, 2 * pr + i, kb * P:T], start=True, stop=False)
                            op = pe.matmul(ps[:, st_bank(m) + i, at:at + P], identb[:], mask_kq[:], start=False, stop=True)
                        op.then_inc(st_ps, 1)

                def maxima_T(g):
                    pe.wait_ge(nmc_rdy, b * G + g + 1)
                    if g == 0:
                        pe.wait_ge(va_sb, b * TB + 3)
                    else:
                        pe.wait_ge(nmrow_rdy, b * G + g)
                    if g >= 2:
                        pe.wait_ge(pvT_used, b * G + g - 1)
                    for qb in range(TB):
                        op = pe.transpose(ps[0:8, TPB, blk(qb)], nmc[:, qb, :], ident[:])
                    op.then_inc(nm_ps, 1)

                def weigh(g):
                    pe.wait_ge(exp_rdy, 2 * (b * STEPS + 6 * g + 6))
                    if g == 0:
                        pe.wait_ge(va_sb, (b + 1) * TB)
                    else:
                        pe.wait_ge(pvs_rdy, b * G + g)
                    for kb in range(TB):
                        w = T - kb * P
                        for j in range(4):
                            op = pe.matmul(ps[quad(j), 6, kb * P:T], v_aug[:, kb, 4 * g + j, :], e_row[g % 2][:, j, E_AT[kb]:E_AT[kb] + w],
                                           start=kb == 0, stop=kb == TB - 1)
                    op.then_inc(pv_ps, 1)

                def weighed_T(g):
                    pe.wait_ge(pvs_rdy, b * G + g + 1)
                    pe.wait_ge(nmrow_rdy, b * G + min(g + 2, G))
                    if g == G - 1:
                        pe.wait_ge(pvT_used, b * G + g)
                    for qb in range(TB):
                        op = pe.transpose(ps[:, TPB, blk(qb)], pvs[:, blk(qb)], ident[:])
                    op.then_inc(pvT_ps, 1)

                def gate(f, dbs=range(DB)):
                    if 0 in dbs:
                        if f == 0:
                            pe.wait_ge(qk_lo, (b + 1) * 2 * G)
                        elif f >= 2:
                            pe.wait_ge(prod_rdy, b * NF + f - 1)
                        pe.wait_ge(gu_lo, b * NF + f + 1)
                    for db in dbs:
                        split_matmul(ps[:, 4 + (2 * f) % 3, :], gu_s[f % 2][0][:, blk(db)], gu_s[f % 2][1][:, blk(db)],
                                     h_s[0][:, db, :], h_s[1][:, db, :], db == 0, False)

                def gate_mod(f):
                    if f == 0:
                        pe.wait_ge(base_free, 64)
                        pe.wait_ge(tT_rdy, b + 1)
                    pe.matmul(ps[:, 4 + (2 * f) % 3, :], b_s[:, blk(f)], t_s[:], start=False, stop=True).then_inc(gate_ps, 1)

                def up(f, dbs=range(DB)):
                    if f >= 1:
                        pe.wait_ge(gsil_rdy, b * NF + f)
                    for db in dbs:
                        op = split_matmul(ps[:, 4 + (2 * f + 1) % 3, :], gu_s[f % 2][0][:, D + db * P:D + (db + 1) * P],
                                          gu_s[f % 2][1][:, D + db * P:D + (db + 1) * P],
                                          h_s[0][:, db, :], h_s[1][:, db, :], db == 0, db == DB - 1)
                    if DB - 1 in dbs:
                        op.then_inc(up_ps, 1)

                def down(f):
                    pe.wait_ge(act_lo, b * NF + f + 1)
                    pe.wait_ge(wd_lo, b * NF + f + 1)
                    for tb in range(TB):
                        op = split_matmul(ps[:, tb, :], act_s[f % 2][0][:, blk(tb)], act_s[f % 2][1][:, blk(tb)],
                                          wd_s[f % 2][0][:], wd_s[f % 2][1][:], f == 0, f == NF - 1)
                        if f == NF - 1:
                            op.then_inc(mlp_ps, 1)
                    if f < NF - 1:
                        op.then_inc(down_ps, 1)

                pe.wait_ge(hn_lo, (b + 1) * DB)
                project(0, 0)
                project(0, 1)
                pe.wait_ge(ga_lo, DB)
                values(0)
                values(1)
                for n in range(min(PROJ_AT.values()), STEPS + LAG):
                    if n % 6 == 0 and 6 <= n <= STEPS:
                        maxima_T(n // 6 - 1)
                    if 0 <= n < STEPS:
                        scores(n)
                    for g, at in PROJ_AT.items():
                        if at <= n < at + 4:
                            project(g, (n - at) // 2, ((0, 1), (2, 3))[(n - at) % 2])
                    for tb, at in VALUE_AT.items():
                        if n == at:
                            values(tb)
                    m = n - LAG
                    if m == STEPS - 6:
                        gate(0)
                    if m >= 0:
                        scores_T(m)
                    if m >= 6 and m % 6 == 0:
                        weigh(m // 6 - 1)
                    if m >= 7 and m % 6 == 1:
                        weighed_T(m // 6 - 1)
                    if m in (STEPS - 4, STEPS - 2):
                        up(0, ((m - STEPS + 4) // 2,))
                up(0, (2,))
                weigh(G - 1)
                weighed_T(G - 1)
                gate(1, (0, 1, 2))
                pe.wait_ge(t_rdy, b + 1)
                for tb in range(TB):
                    op = pe.transpose(ps[0:5 * R, TPB, blk(tb)], tcols[:, tb, :], ident[:])
                op.then_inc(tT_ps, 1)
                up(0, (3,))
                gate_mod(0)
                gate(1, (3,))
                gate_mod(1)

                for f in range(NF):
                    if f >= 2:
                        gate(f)
                        gate_mod(f)
                    if f >= 1:
                        up(f)
                    if not last and f in KEYS_AT:
                        keys_T(b + 1, KEYS_AT.index(f))
                    if not last and Y_AT <= f < Y_AT + TB:
                        rows_y(b + 1, f - Y_AT)
                    if not last and f == NF - 1:
                        pe.wait_ge(prod_rdy, b * NF + f)
                        for db in (0, 1):
                            normed_T(b + 1, db)
                    if f >= 1:
                        down(f - 1)
                if not last:
                    pe.wait_ge(prod_rdy, (b + 1) * NF)
                    for db in (2, 3):
                        normed_T(b + 1, db)
                down(NF - 1)

            with pe.Fori(0, NB - 1) as b:
                batch(b, False)
            batch(NB - 1, True)


def kernel(x, ctx_2048, g_xattn, g_ffn, L0_xattn_w, L0_xattn_u, L0_ffn_ln1_w, L0_ffn_ln2_w, L0_ffn_Wq, L0_ffn_Wk,
           L0_ffn_Wv, L0_ffn_Wo, L0_ffn_A, L0_ffn_B, L0_ffn_W_in_base, L0_ffn_W_up_base, L0_ffn_W_down):
    from concourse import bacc
    from concourse.bass_utils import run_bass_kernel_spmd

    a = np.asarray
    col = lambda v: np.ascontiguousarray(a(v).reshape(DB, P).T)
    tiles = lambda m: a(m).reshape(NF, P, DB, P).transpose(0, 3, 2, 1)
    w_gu = np.ascontiguousarray(np.stack([tiles(L0_ffn_W_in_base), tiles(L0_ffn_W_up_base)], axis=2).reshape(NF, P, 2 * D))
    arrays = {
        "x": a(x),
        "ctxT": np.ascontiguousarray(a(ctx_2048).transpose(0, 2, 1)),
        "w4": col(L0_xattn_w), "u4": col(L0_xattn_u),
        "gates": np.ascontiguousarray(np.broadcast_to(np.concatenate([a(g_xattn), a(g_ffn)])[None, :], (P, 2))),
        "ln1": col(L0_ffn_ln1_w), "ln2": col(L0_ffn_ln2_w),
        "wqT": np.ascontiguousarray(a(L0_ffn_Wq).T), "wkT": np.ascontiguousarray(a(L0_ffn_Wk).T),
        "wv": a(L0_ffn_Wv), "wo": a(L0_ffn_Wo), "a4": a(L0_ffn_A), "b_mod": a(L0_ffn_B),
        "w_gu": w_gu, "w_down": np.ascontiguousarray(a(L0_ffn_W_down).T),
    }
    arrays = {f"{k}_dram": np.ascontiguousarray(v) for k, v in arrays.items()}
    nc = bacc.Bacc("TRN2", target_bir_lowering=False, num_devices=1, dynamic_dma_scratch_size=DGE_SCRATCH)
    args = [nc.dram_tensor(k, v.shape, F32, kind="ExternalInput").ap() for k, v in arrays.items()]
    args.append(nc.dram_tensor("out_dram", (NB, T, D), F32, kind="ExternalOutput").ap())
    flamingo_layer(nc, *args)
    return run_bass_kernel_spmd(nc, [arrays], core_ids=[0]).results[0]["out_dram"]
```
